# Optimizing a Trainium2 kernel written in Bass

```python
import numpy as np
import jax
import jax.numpy as jnp

def _softmax(x, axis=-1):
    return jax.nn.softmax(x, axis=axis)

def _gelu(x):
    return jax.nn.gelu(x, approximate=True)

def _silu(x):
    return jax.nn.silu(x)

def _sigmoid(x):
    return jax.nn.sigmoid(x)

def _layernorm(x, axis=-1, eps=1e-05):
    m = jnp.mean(x, axis=axis, keepdims=True)
    v = jnp.var(x, axis=axis, keepdims=True)
    return (x - m) / jnp.sqrt(v + eps)

def _scatter_add(tgt, idx, src, axis=0):
    return tgt.at[idx].add(src)

def _segment_sum(src, seg, n):
    return jax.ops.segment_sum(src, seg, n)
kernel_name = 'mk_xattn_ffn_d1_seqx_r2_ed757e'

def setup_inputs(seed: int=0):
    np.random.seed(seed)
    _w = jnp.asarray

    def _rec_inputs():
        import jax
        import jax.numpy as jnp
        _rk = jax.random.key(seed)
        x = 0.0003765 + 1 * jax.random.normal(jax.random.fold_in(_rk, 1), (16, 512, 1024), jnp.float32)
        _lenS = 512 - jax.random.randint(jax.random.fold_in(_rk, 7), (16,), 0, max(1, 512 // 4) + 1, jnp.int32)
        _lenS2 = 512 - jax.random.randint(jax.random.fold_in(_rk, 8), (16,), 0, max(1, 512 // 4) + 1, jnp.int32)
        _ctx_2048P = jax.random.normal(jax.random.fold_in(_rk, 11), (16, 16, 1024), jnp.float32)
        _ctx_2048c = jax.random.dirichlet(jax.random.fold_in(_rk, 511), 0.3 * jnp.ones((16,), jnp.float32), (16, 512))
        _ctx_2048t = jnp.einsum('bsk,bkd->bsd', _ctx_2048c, _ctx_2048P)
        _ctx_2048t = _ctx_2048t * jax.lax.rsqrt(jnp.mean(jnp.square(_ctx_2048t)) + 1e-12) * 0.953939
        ctx_2048 = -0.000292821 + 1.00034 * (_ctx_2048t + 0.3 * jax.random.normal(jax.random.fold_in(_rk, 611), (16, 512, 1024), jnp.float32))
        return (x, ctx_2048)
    x, ctx_2048 = _rec_inputs()

    def _L0_xattn_setup():
        import jax, jax.numpy as jnp
        import numpy as np
        key = jax.random.key(seed)
        k1, k2, k3, k4, k5 = jax.random.split(key, 5)
        B, D_MODEL, L = (2, 512, 1024)
        HEAD_DIM = 8
        H = D_MODEL // HEAD_DIM
        return {'k': jax.random.normal(k1, (B, D_MODEL, L), dtype=jnp.float32), 'v': jax.random.normal(k2, (B, D_MODEL, L), dtype=jnp.float32), 'q': jax.random.normal(k3, (B, D_MODEL, L), dtype=jnp.float32), 'ssm_kernel': jax.random.normal(k4, (H, L), dtype=jnp.float32), 'D': jax.random.normal(k5, (H,), dtype=jnp.float32), 'head_dim': HEAD_DIM}
    _L0_xattn_all = _L0_xattn_setup()
    _L0_xattn_in = {k: v for k, v in _L0_xattn_all.items() if k in ('ssm_kernel', 'D')}
    del _L0_xattn_all

    def _L0_ffn_setup():
        import jax, jax.numpy as jnp
        import numpy as np
        B, S, H = (2, 1024, 1024)
        E, G, TKG, K = (32, 8, 4, 8)
        I, SI = (512, 1024)
        ROUTED_SCALE = 2.5

        def _moe_forward(hidden_states, router_w, router_bias, w_gate, w_up, w_down, sw_gate, sw_up, sw_down):
            x = hidden_states.reshape(-1, H)
            T = x.shape[0]
            logits = x.astype(jnp.float32) @ router_w.astype(jnp.float32)
            scores = jax.nn.sigmoid(logits)
            scores_grouped = (scores + router_bias).reshape(T, G, E // G)
            top2, _ = jax.lax.top_k(scores_grouped, 2)
            group_scores = top2.sum(-1)
            _, top_groups = jax.lax.top_k(group_scores, TKG)
            mask = jnp.ones((T, G), bool).at[jnp.arange(T)[:, None], top_groups].set(False)
            masked = jnp.where(mask[:, :, None], 0.0, scores_grouped).reshape(T, E)
            _, top_k_index = jax.lax.top_k(masked, K)
            tkw = jnp.take_along_axis(scores, top_k_index, axis=-1)
            tkw = tkw / tkw.sum(-1, keepdims=True)
            tkw = (tkw * ROUTED_SCALE).astype(hidden_states.dtype)
            flat_idx = top_k_index.reshape(-1)
            sort_idx = jnp.argsort(flat_idx)
            xs = jnp.repeat(x, K, axis=0)[sort_idx]
            group_sizes = jnp.bincount(flat_idx, length=E).astype(jnp.int32)
            gate = jax.lax.ragged_dot(xs, w_gate, group_sizes)
            up = jax.lax.ragged_dot(xs, w_up, group_sizes)
            down = jax.lax.ragged_dot(jax.nn.silu(gate) * up, w_down, group_sizes)
            unsort = jnp.argsort(sort_idx)
            routed = (down[unsort].reshape(T, K, H) * tkw[..., None]).sum(axis=1)
            shared = jax.nn.silu(x @ sw_gate) * (x @ sw_up) @ sw_down
            return (routed + shared).reshape(hidden_states.shape)
        key = jax.random.key(seed)
        ks = jax.random.split(key, 9)

        def w(k, shape, fan_in):
            return jax.random.normal(k, shape, jnp.float32) / np.float32(np.sqrt(fan_in))
        return dict(hidden_states=jax.random.normal(ks[0], (B, S, H), jnp.float32), router_w=w(ks[1], (H, E), H), router_bias=jnp.zeros((E,), jnp.float32), w_gate=w(ks[2], (E, H, I), H), w_up=w(ks[3], (E, H, I), H), w_down=w(ks[4], (E, I, H), I), sw_gate=w(ks[5], (H, SI), H), sw_up=w(ks[6], (H, SI), H), sw_down=w(ks[7], (SI, H), SI))
    _L0_ffn_all = _L0_ffn_setup()
    _L0_ffn_in = {k: v for k, v in _L0_ffn_all.items() if k in ('router_w', 'router_bias', 'w_gate', 'w_up', 'w_down', 'sw_gate', 'sw_up', 'sw_down')}
    del _L0_ffn_all
    return {'x': x, 'ctx_2048': ctx_2048, 'L0_xattn_ssm_kernel': _L0_xattn_in['ssm_kernel'], 'L0_xattn_D': _L0_xattn_in['D'], 'L0_ffn_router_w': _L0_ffn_in['router_w'], 'L0_ffn_router_bias': _L0_ffn_in['router_bias'], 'L0_ffn_w_gate': _L0_ffn_in['w_gate'], 'L0_ffn_w_up': _L0_ffn_in['w_up'], 'L0_ffn_w_down': _L0_ffn_in['w_down'], 'L0_ffn_sw_gate': _L0_ffn_in['sw_gate'], 'L0_ffn_sw_up': _L0_ffn_in['sw_up'], 'L0_ffn_sw_down': _L0_ffn_in['sw_down']}

def reference(x, ctx_2048, L0_xattn_ssm_kernel, L0_xattn_D, L0_ffn_router_w, L0_ffn_router_bias, L0_ffn_w_gate, L0_ffn_w_up, L0_ffn_w_down, L0_ffn_sw_gate, L0_ffn_sw_up, L0_ffn_sw_down):
    import jax
    import jax.numpy as jnp

    def _L0_xattn_ref(k, v, q, ssm_kernel, D, head_dim):
        import jax, jax.numpy as jnp
        import numpy as np
        B, HD, L = k.shape
        H = HD // head_dim
        fft_size = 2 * L
        k_ = k.reshape(B, H, head_dim, L)
        v_ = v.reshape(B, H, head_dim, L)
        q_ = q.reshape(B, H, head_dim, L)
        kv = jnp.einsum('bhil,bhjl->bijhl', k_, v_)
        kv_f = jnp.fft.rfft(kv, n=fft_size)
        kernel_f = jnp.fft.rfft(ssm_kernel, n=fft_size)
        y = jnp.fft.irfft(kv_f * kernel_f, n=fft_size)[..., :L]
        out = y + kv * D[None, None, None, :, None]
        out = jnp.einsum('bijhl,bhil->bjhl', out, q_)
        out = jnp.transpose(out, (0, 2, 1, 3)).reshape(B, H * head_dim, L)
        return out.astype(k.dtype)

    def _L0_ffn_ref(hidden_states, router_w, router_bias, w_gate, w_up, w_down, sw_gate, sw_up, sw_down):
        import jax, jax.numpy as jnp
        import numpy as np
        B, S, H = (2, 1024, 1024)
        E, G, TKG, K = (32, 8, 4, 8)
        I, SI = (512, 1024)
        ROUTED_SCALE = 2.5

        def _moe_forward(hidden_states, router_w, router_bias, w_gate, w_up, w_down, sw_gate, sw_up, sw_down):
            x = hidden_states.reshape(-1, H)
            T = x.shape[0]
            logits = x.astype(jnp.float32) @ router_w.astype(jnp.float32)
            scores = jax.nn.sigmoid(logits)
            scores_grouped = (scores + router_bias).reshape(T, G, E // G)
            top2, _ = jax.lax.top_k(scores_grouped, 2)
            group_scores = top2.sum(-1)
            _, top_groups = jax.lax.top_k(group_scores, TKG)
            mask = jnp.ones((T, G), bool).at[jnp.arange(T)[:, None], top_groups].set(False)
            masked = jnp.where(mask[:, :, None], 0.0, scores_grouped).reshape(T, E)
            _, top_k_index = jax.lax.top_k(masked, K)
            tkw = jnp.take_along_axis(scores, top_k_index, axis=-1)
            tkw = tkw / tkw.sum(-1, keepdims=True)
            tkw = (tkw * ROUTED_SCALE).astype(hidden_states.dtype)
            flat_idx = top_k_index.reshape(-1)
            sort_idx = jnp.argsort(flat_idx)
            xs = jnp.repeat(x, K, axis=0)[sort_idx]
            group_sizes = jnp.bincount(flat_idx, length=E).astype(jnp.int32)
            gate = jax.lax.ragged_dot(xs, w_gate, group_sizes)
            up = jax.lax.ragged_dot(xs, w_up, group_sizes)
            down = jax.lax.ragged_dot(jax.nn.silu(gate) * up, w_down, group_sizes)
            unsort = jnp.argsort(sort_idx)
            routed = (down[unsort].reshape(T, K, H) * tkw[..., None]).sum(axis=1)
            shared = jax.nn.silu(x @ sw_gate) * (x @ sw_up) @ sw_down
            return (routed + shared).reshape(hidden_states.shape)
        return _moe_forward(hidden_states, router_w, router_bias, w_gate, w_up, w_down, sw_gate, sw_up, sw_down)
    x = x + _L0_xattn_ref(ctx_2048, ctx_2048, _layernorm(x, axis=-1), L0_xattn_ssm_kernel, L0_xattn_D, 8)
    x = x + _L0_ffn_ref(_layernorm(x, axis=-1), L0_ffn_router_w, L0_ffn_router_bias, L0_ffn_w_gate, L0_ffn_w_up, L0_ffn_w_down, L0_ffn_sw_gate, L0_ffn_sw_up, L0_ffn_sw_down)
    return x

_drawn_inputs = setup_inputs


def setup_inputs(seed=0):
    import zlib

    import numpy as np

    out = dict(_drawn_inputs(seed))
    spreads = {'L0_ffn_router_bias': (0.0, 0.8)}
    factors = {'L0_ffn_router_w': 8.0,
     'L0_ffn_w_gate': 8.0,
     'L0_ffn_w_up': 8.0,
     'L0_ffn_w_down': 8.0,
     'L0_ffn_sw_gate': 7.808,
     'L0_ffn_sw_up': 7.334,
     'L0_ffn_sw_down': 7.331}
    for name, (base, spread) in spreads.items():
        noise = np.random.default_rng([zlib.crc32(name.encode()), seed]).standard_normal(out[name].shape)
        drawn = base * np.exp(spread * noise) if base else spread * noise
        out[name] = jnp.asarray(drawn.astype(out[name].dtype))
    for name, factor in factors.items():
        out[name] = (out[name] * factor).astype(out[name].dtype)
    return out
```

```python
import concourse.bass as bass
from concourse import mybir
from contextlib import ExitStack

F32 = mybir.dt.float32
F32R = mybir.dt.float32r
I32 = mybir.dt.int32
ALU = mybir.AluOpType
ACT = mybir.ActivationFunctionType
AXX = mybir.AxisListType.X

P = 128
B, CH, L = 16, 512, 1024
HD = 8
HEADS = CH // HD
PAIRS = HD * (HD + 1) // 2
LB = L // P
CG = 32
HPG = CG // HD
BT = P // CG
TPG = B // BT
NTOK = B * CH
NTILE = NTOK // P
NH = B // 2 * PAIRS
EPS = 1e-5

E, EG, GSZ, TKG, K = 32, 8, 4, 4, 8
I, SI = 512, 1024
SCALE = 2.5
RB = 8
LIST = NTOK
LROWS = LIST // P
EXPERT_TILES = NTOK * K // P + E
SH0 = EXPERT_TILES
SH1 = SH0 + NTILE
TILES = SH1 + NTILE
TCOLS = -(-TILES // P)
NE = E + SI // I
GU, DN = 4, 2
UNITS = GU + DN

C_ID, C_REV, C_TRI, C_ONE = 0, 128, 256, 384
C_GT = 512
C_EB = C_GT + EG * EG
C_TOK = C_EB + E
C_T = C_TOK + RB
C_EPS = C_T + TCOLS
C_N = C_EPS + 1

F_EXPERT, F_FIRST, F_ROW, F_START, F_END = range(5)
FIELDS = 5


def constants():
    import numpy as np
    c = np.zeros((P, C_N), np.float32)
    p = np.arange(P)
    c[p, C_ID + p] = 1
    c[p, C_REV + P - 1 - p] = 1
    c[:, C_TRI:C_TRI + P] = p[:, None] < p[None, :]
    c[:, C_ONE:C_ONE + P] = 1
    g = np.arange(EG)
    c[:, C_GT:C_GT + EG * EG] = (g[None, :] < g[:, None]).reshape(1, -1)
    c[:, C_EB:C_EB + E] = LIST * np.arange(E)
    c[:, C_TOK:C_TOK + RB] = p[:, None] + P * np.arange(RB)
    c[:, C_T:C_T + TCOLS] = p[:, None] + P * np.arange(TCOLS)
    c[:, C_EPS] = EPS
    return c, np.arange(NTOK, dtype=np.int32).reshape(NTOK, 1)


class Chain:

    def __init__(self, sem):
        self.sem, self.n = sem, 0

    def link(self, eng, ins):
        ins.then_inc(self.sem, 1)
        self.n += 1
        eng.wait_ge(self.sem, self.n)

    def restart(self, eng):
        eng.sem_clear(self.sem)
        self.n = 0


class Step:

    def __init__(self, block, u):
        self.block, self.u = block, u

    def n(self, k):
        return 8 * self.block + (self.u - k)

    def half(self, k):
        return 4 * self.block + (self.u - k) // 2

    def group(self, k):
        return 2 * self.block + (self.u - k) // 4

    def slot(self, k):
        return (self.u - k) % 2

    def quarter(self, k):
        return (self.u - k) % 4

    def gslot(self, k):
        return (self.u - k) // 4 % 2

    def on(self, k):
        return not isinstance(self.block, int) or 0 <= self.n(k) < 64

    def past(self, k):
        return self.n(k) if not isinstance(self.block, int) else min(max(self.n(k), 0), 64)


NORM, INS, TOEP, KVS, CONV, SECOND, OUT, ROUTE = 0, 1, 4, 4, 5, 6, 9, 10
LOOPED = (2, 8)
BLOCKS = 10
STEPS = 74


def walk(eng, step, chain=None):
    for block in range(LOOPED[0]):
        for u in range(8):
            step(Step(block, u))
    with eng.Fori(0, LOOPED[1] - LOOPED[0]) as turn:
        block = turn + LOOPED[0]
        if chain:
            chain.restart(eng)
        for u in range(8):
            step(Step(block, u))
    if chain:
        chain.restart(eng)
    for block in range(LOOPED[1], BLOCKS):
        for u in range(8):
            if 8 * block + u < STEPS:
                step(Step(block, u))


def wait(eng, sem, value):
    if not isinstance(value, int) or value > 0:
        eng.wait_ge(sem, value)


def settle(pool, turns):
    pool.sem_inc(turns, 1)


def channel_rows(t, group, quarter):
    v = t.rearrange("(q b) (g c) l -> g q c b l", b=BT, c=CG)
    return v[bass.ds(group, 1), quarter].rearrange("o c b l -> (o c) b l")


def batch_rows(t, group, batch):
    return t[batch, bass.ds(group * CG, CG), :]


def mix_and_route(nc, A, keep):
    x, ctx, kern, dvec, rw, bias = A["x"], A["ctx"], A["kern"], A["dvec"], A["rw"], A["bias"]
    kpad, x2d, xnd, lists = A["kpad"], A["x2d"], A["xnd"], A["lists"]
    es = ExitStack()
    with es:
        def sb(name, shape, dt=F32):
            return es.enter_context(nc.sbuf_tensor(name, shape, dt))

        def sem(name):
            return es.enter_context(nc.semaphore(name))

        kT = [sb(f"kT{i}", [P, LB * B, CG]) for i in range(2)]
        qT = [sb(f"qT{i}", [P, LB * B, CG]) for i in range(2)]
        kv = [sb(f"kv{i}", [P, LB * B, PAIRS]) for i in range(2)]
        ysb = sb("ysb", [P, LB * B, PAIRS])
        prod = sb("prod", [P, LB * B // 2, HD, HD])
        traw = [sb(f"traw{i}", [P, L]) for i in range(2)]
        toep = [sb(f"toep{i}", [P, L]) for i in range(2)]
        xin = [sb(f"xin{i}", [P, L]) for i in range(2)]
        cin = [sb(f"cin{i}", [P, L]) for i in range(2)]
        xres = [sb(f"xres{i}", [P, L]) for i in range(2)]
        xn2 = [sb(f"xn2{i}", [P, L]) for i in range(2)]
        x2T = sb("x2T", [P, LB, P])
        rws = sb("rws", [P, LB, E])
        biasb = sb("biasb", [P, E])
        st_in = sb("st_in", [P, 2, 6])
        mv_in = sb("mv_in", [P, 2])
        sd_in = sb("sd_in", [P, 2])
        st_out = sb("st_out", [P, 2, 6])
        mv_out = sb("mv_out", [P, 2])
        sd_out = sb("sd_out", [P, 2])
        lg = sb("lg", [P, RB, E])
        sc = sb("sc", [P, RB, E])
        sb_ = sb("sbias", [P, RB, E])
        msk = sb("msk", [P, RB, E])
        rep = sb("rep", [P, RB, E])
        chosen = sb("chosen", [P, RB, E])
        wn = sb("wn", [P, RB, E])
        key = sb("key", [P, RB, E])
        runs = sb("runs", [P, RB + 1, E])
        pm = sb("pm", [P, RB * EG, 4])
        gs = sb("gs", [P, RB, EG])
        gsel = sb("gsel", [P, RB, EG])
        top = sb("top", [P, RB, K])
        ws = sb("ws", [P, RB])
        tokf = sb("tokf", [P, RB])
        toki = sb("toki", [P, RB], I32)
        place = sb("place", [P, RB, K], I32)
        con, vslot, wpick, cnt = keep["con"], keep["vslot"], keep["wpick"], keep["cnt"]
        ident = con[:, C_ID:C_ID + P]
        kp = ysb[0:HEADS, :, :].rearrange("p a b -> p (a b)")[:, 0:P + L]
        zero_i = prod[:, 0:E, :, :].rearrange("p a b c -> p (a b c)").bitcast(I32)
        wide = prod[:, :, :, :].rearrange("p a b c -> p (a b c)")[:, 0:RB * K * E]\
            .rearrange("p (t k e) -> p t k e", t=RB, k=K)
        cmp8 = prod[:, :, :, :].rearrange("p a b c -> p (a b c)")[:, 0:2 * RB * EG * EG]\
            .rearrange("p (s t g h) -> p s t g h", s=2, t=RB, g=EG)

        yps = [es.enter_context(nc.psum_tensor(f"yps{i}", [P, 2, 512], F32)) for i in range(2)]
        ps0 = es.enter_context(nc.psum_tensor("ps0", [P, 2 * 512], F32))
        ps1 = es.enter_context(nc.psum_tensor("ps1", [P, 2 * 512], F32))

        setup_ld, kp_zero, kp_ready = sem("setup_ld"), sem("kp_zero"), sem("kp_ready")
        kpad_st, lists_st = sem("kpad_st"), sem("lists_st")
        x_ld, c_ld = [sem(f"x_ld{i}") for i in range(2)], [sem(f"c_ld{i}") for i in range(2)]
        t_ld, r_ld = [sem(f"t_ld{i}") for i in range(2)], [sem(f"r_ld{i}") for i in range(2)]
        x2_st, xn_st = [sem(f"x2_st{i}") for i in range(2)], [sem(f"xn_st{i}") for i in range(2)]
        var_in, sqrt_in, normed = sem("var_in"), sem("sqrt_in"), sem("normed")
        var_out, sqrt_out, normed2 = sem("var_out"), sem("sqrt_out"), sem("normed2")
        toep_mm, toep_copied = sem("toep_mm"), sem("toep_copied")
        xin_mm, xin_copied = sem("xin_mm"), sem("xin_copied")
        ctx_mm, ctx_copied = sem("ctx_mm"), sem("ctx_copied")
        kv_built, conv_done = sem("kv_built"), sem("conv_done")
        y_mm, y_copied = sem("y_mm"), sem("y_copied")
        first_half, second_half = sem("first_half"), sem("second_half")
        out_mm, out_added = sem("out_mm"), sem("out_added")
        x2T_mm, x2T_copied = sem("x2T_mm"), sem("x2T_copied")
        lg_mm, lg_copied, scored = sem("lg_mm"), sem("lg_copied"), sem("scored")
        chose, rank_mm, rank_used = sem("chose"), sem("rank_mm"), sem("rank_used")
        placed, listed, place_free = sem("placed"), sem("listed"), sem("place_free")
        dve_seq, pool_turns = sem("dve_seq"), sem("pool_turns")

        block = es.enter_context(nc.Block())

        @block.sync
        def _(sp):
            sp.dma_start(kp[:, P - 1:P - 1 + L], kern).then_inc(setup_ld, 16)
            sp.dma_start(sd_in[0:HEADS, 0:1], dvec.rearrange("(h o) -> h o", o=1)).then_inc(setup_ld, 16)
            sp.dma_start(con[:, :], A["con"]).then_inc(setup_ld, 16)
            sp.dma_start(rws[:, :, :], rw.rearrange("(k p) e -> p k e", p=P)).then_inc(setup_ld, 16)
            sp.dma_start(biasb[:, :], bias.rearrange("(o e) -> o e", o=1).to_broadcast([P, E]))\
                .then_inc(setup_ld, 16)
            sp.wait_ge(kp_zero, 2)
            sp.dma_start(lists[0:E * LIST, :].rearrange("(p n) o -> p (n o)", p=P), zero_i)\
                .then_inc(lists_st, 16)
            sp.dma_start(lists[E * LIST:, :].rearrange("(p n) o -> p (n o)", p=P),
                         A["tokens"].rearrange("(p n) o -> p (n o)", p=P)).then_inc(lists_st, 16)
            sp.wait_ge(kp_ready, 1)
            sp.dma_start(kpad, kp).then_inc(kpad_st, 16)
            sp.wait_ge(kpad_st, 16)

            def step(s):
                if s.on(NORM):
                    wait(sp, xin_mm, s.past(NORM + 1))
                    sp.dma_start(xin[s.slot(NORM)][:, :],
                                 channel_rows(x, s.group(NORM), s.quarter(NORM)))\
                        .then_inc(x_ld[s.slot(NORM)], 16)
                    wait(sp, ctx_mm, s.past(NORM + 1))
                    sp.dma_start(cin[s.slot(NORM)][:, :],
                                 channel_rows(ctx, s.group(NORM), s.quarter(NORM)))\
                        .then_inc(c_ld[s.slot(NORM)], 16)
                k = TOEP - 1
                if s.on(k):
                    wait(sp, toep_mm, s.past(k + 1))
                    src = bass.AP(tensor=kpad.tensor, offset=s.n(k) * (L + P),
                                  ap=[[1, P], [1, L]])
                    sp.dma_start(traw[s.slot(k)][:, :], src).then_inc(t_ld[s.slot(k)], 16)
                k = OUT - 1
                if s.on(k):
                    wait(sp, x2_st[s.slot(k)], 16 * s.half(k))
                    for b in range(BT):
                        sp.dma_start(xres[s.slot(k)][b * CG:(b + 1) * CG, :],
                                     batch_rows(x, s.group(k), s.quarter(k) * BT + b))\
                            .then_inc(r_ld[s.slot(k)], 16)

            walk(sp, step)

        @block.gpsimd
        def _(pool):
            def step(s):
                if s.on(OUT):
                    pool.wait_ge(normed2, s.n(OUT) + 1)
                    pool.dma_start(x2d[bass.ds(s.n(OUT) * P, P), :], xres[s.slot(OUT)][:, :])\
                        .then_inc(x2_st[s.slot(OUT)], 16)
                    pool.dma_start(xnd[bass.ds(s.n(OUT) * P, P), :], xn2[s.slot(OUT)][:, :])\
                        .then_inc(xn_st[s.slot(OUT)], 16)
                if routes(s, 2):
                    list_tokens(s.block - 2)

            def list_tokens(r):
                pool.wait_ge(placed, r + 1)
                settle(pool, pool_turns)
                for t in range(RB):
                    for k in range(K):
                        pool.indirect_dma_start(
                            out=lists, out_offset=bass.IndirectOffsetOnAxis(ap=place[:, t, k:k + 1], axis=0),
                            in_=toki[:, t:t + 1], in_offset=None).then_inc(listed, 16)
                pool.wait_ge(listed, 16 * RB * K * (r + 1))
                pool.sem_inc(place_free, 1)

            pool.sem_inc(place_free, 1)
            pool.wait_ge(lists_st, 32)
            walk(pool, step)
            list_tokens(NTILE // RB - 1)
            for i in range(2):
                pool.wait_ge(x2_st[i], 16 * NTILE // 2)
                pool.wait_ge(xn_st[i], 16 * NTILE // 2)

        @block.scalar
        def _(act):
            def copy_y(s, lb):
                if not s.on(CONV):
                    return
                n = s.n(CONV)
                if lb == 0:
                    wait(act, first_half, n)
                if lb == LB // 2:
                    wait(act, second_half, n)
                act.wait_ge(y_mm, 8 * n + lb + 1)
                act.activation(ysb[:, lb * B:(lb + 1) * B, :].rearrange("p (h b) m -> p h (b m)", h=2),
                               yps[lb % 2][:, :, 0:NH], ACT.Copy).then_inc(y_copied, 1)

            def copy_tile(s, ps, dst):
                q = s.quarter(INS)
                v = dst[s.gslot(INS)][:, :, :].rearrange("p (m b) c -> p m b c", m=LB)
                return act.activation(v[:, :, q * BT:(q + 1) * BT, :],
                                      ps[:, :].rearrange("p (m c b) -> p m b c", m=LB, b=BT), ACT.Copy)

            def step(s):
                if s.on(TOEP):
                    n = s.n(TOEP)
                    act.wait_ge(toep_mm, n + 1)
                    wait(act, conv_done, s.past(TOEP + 1) if isinstance(n, int) else n - 1)
                    act.activation(toep[s.slot(TOEP)][:, :], ps0[:, :], ACT.Copy).then_inc(toep_copied, 1)
                for lb in range(3):
                    copy_y(s, lb)
                if s.on(NORM):
                    act.wait_ge(var_in, s.n(NORM) + 1)
                    act.activation(sd_in[:, 0:1], mv_in[:, 1:2], ACT.Sqrt,
                                   bias=con[:, C_EPS:C_EPS + 1]).then_inc(sqrt_in, 1)
                for lb in range(3, 5):
                    copy_y(s, lb)
                if s.on(INS):
                    act.wait_ge(xin_mm, s.n(INS) + 1)
                    copy_tile(s, ps0, qT).then_inc(xin_copied, 1)
                copy_y(s, 5)
                if s.on(INS):
                    act.wait_ge(ctx_mm, s.n(INS) + 1)
                    if not isinstance(s.block, int) or s.group(INS) >= 2:
                        act.wait_ge(kv_built, HPG * (s.group(INS) - 1))
                    copy_tile(s, ps1, kT).then_inc(ctx_copied, 1)
                if s.on(OUT):
                    act.wait_ge(var_out, s.n(OUT) + 1)
                    act.activation(sd_out[:, 0:1], mv_out[:, 1:2], ACT.Sqrt,
                                   bias=con[:, C_EPS:C_EPS + 1]).then_inc(sqrt_out, 1)
                if s.on(ROUTE):
                    act.wait_ge(x2T_mm, s.n(ROUTE) + 1)
                    act.activation(x2T[:, :, :].rearrange("p k t -> p (k t)"), ps0[:, :], ACT.Copy)\
                        .then_inc(x2T_copied, 1)
                copy_y(s, 6)
                if s.on(ROUTE):
                    act.wait_ge(lg_mm, s.n(ROUTE) + 1)
                    act.activation(lg[:, (s.u - ROUTE) % RB, :], ps1[:, 0:E], ACT.Copy)\
                        .then_inc(lg_copied, 1)
                copy_y(s, 7)
                if routes(s, 1):
                    act.wait_ge(lg_copied, s.n(ROUTE) + 1)
                    act.activation(sc[:, :, :], lg[:, :, :], ACT.Sigmoid).then_inc(scored, 1)

            act.wait_ge(setup_ld, 80)
            walk(act, step)

        @block.vector
        def _(dve):
            seq = Chain(dve_seq)

            def link(ins):
                seq.link(dve, ins)

            def statistics(src, st, mv):
                dve.bn_stats(st[:, 0, :], src[:, 0:L // 2])
                link(dve.bn_stats(st[:, 1, :], src[:, L // 2:L]))
                return dve.bn_aggr(mv[:, :], st[:, :, :].rearrange("p a b -> p (a b)"))

            def times_queries(s, k, half):
                n, h = s.n(k), s.quarter(k)
                rows = slice(half * LB * B // 2, (half + 1) * LB * B // 2)
                y = ysb[:, rows, :]
                q = qT[s.gslot(k)][:, rows, HD * h:HD * h + HD]
                R = LB * B // 2
                dve.wait_ge(y_copied, 8 * n + (4 if half == 0 else 8))
                if half == 0:
                    dve.wait_ge(xin_copied, TPG * (s.group(k) + 1))
                at = 0
                for i in range(HD):
                    m = HD - i
                    last = dve.tensor_tensor(prod[:, :, i:HD, i], y[:, :, at:at + m],
                                             q[:, :, i:i + 1].to_broadcast([P, R, m]), ALU.mult)
                    if m > 1:
                        last = dve.tensor_tensor(prod[:, :, i, i + 1:HD], y[:, :, at + 1:at + m],
                                                 q[:, :, i + 1:HD], ALU.mult)
                    at += m
                link(last)
                dve.tensor_reduce(q, prod[:, :, :, :], AXX, ALU.add)\
                    .then_inc(second_half if half else first_half, 1)
                dve.wait_ge(second_half if half else first_half, n + 1)

            def step(s):
                if s.on(SECOND):
                    times_queries(s, SECOND, 1)
                if s.on(NORM):
                    n, xt = s.n(NORM), xin[s.slot(NORM)]
                    dve.wait_ge(x_ld[s.slot(NORM)], 16 * (s.half(NORM) + 1))
                    statistics(xt, st_in, mv_in).then_inc(var_in, 1)
                    dve.wait_ge(sqrt_in, n + 1)
                    link(dve.reciprocal(sd_in[:, 1:2], sd_in[:, 0:1]))
                    dve.tensor_scalar(xt[:, :], xt[:, :], mv_in[:, 0:1], sd_in[:, 1:2],
                                      ALU.subtract, ALU.mult).then_inc(normed, 1)
                if s.on(CONV):
                    times_queries(s, CONV, 0)
                if s.on(OUT):
                    n, xr, xo = s.n(OUT), xres[s.slot(OUT)], xn2[s.slot(OUT)]
                    dve.wait_ge(r_ld[s.slot(OUT)], 16 * BT * (s.half(OUT) + 1))
                    dve.wait_ge(out_mm, n + 1)
                    dve.tensor_tensor(xr[:, :], xr[:, :], ps1[:, :], ALU.add).then_inc(out_added, 1)
                    dve.wait_ge(out_added, n + 1)
                    statistics(xr, st_out, mv_out).then_inc(var_out, 1)
                    dve.wait_ge(sqrt_out, n + 1)
                    link(dve.reciprocal(sd_out[:, 1:2], sd_out[:, 0:1]))
                    wait(dve, xn_st[s.slot(OUT)], 16 * s.half(OUT))
                    wait(dve, x2T_mm, s.past(OUT + 1))
                    dve.tensor_scalar(xo[:, :], xr[:, :], mv_out[:, 0:1], sd_out[:, 1:2],
                                      ALU.subtract, ALU.mult).then_inc(normed2, 1)
                if s.on(KVS):
                    n, h = s.n(KVS), s.quarter(KVS)
                    kk = kT[s.gslot(KVS)][:, :, HD * h:HD * h + HD]
                    dve.wait_ge(ctx_copied, TPG * (s.group(KVS) + 1))
                    wait(dve, conv_done, s.past(KVS + 1) if isinstance(n, int) else n - 1)
                    at = 0
                    for i in range(HD):
                        m = HD - i
                        last = dve.tensor_tensor(kv[s.slot(KVS)][:, :, at:at + m], kk[:, :, i:HD],
                                                 kk[:, :, i:i + 1].to_broadcast([P, LB * B, m]), ALU.mult)
                        at += m
                    last.then_inc(kv_built, 1)
                if routes(s, 1):
                    choose(s.block - 2)
                if routes(s, 2):
                    assign(s.block - 2)

            def choose(r):
                dve.wait_ge(scored, r + 1)
                link(dve.tensor_tensor(sb_[:, :, :], sc[:, :, :],
                                       biasb[:, :].rearrange("p (o e) -> p o e", o=1).to_broadcast([P, RB, E]), ALU.add))
                two = sb_[:, :, :].rearrange("p t (g a c) -> p (t g) a c", a=2, c=2)
                dve.tensor_tensor(pm[:, :, 0:2], two[:, :, :, 0], two[:, :, :, 1], ALU.max)
                link(dve.tensor_tensor(pm[:, :, 2:4], two[:, :, :, 0], two[:, :, :, 1], ALU.min))
                g = gs[:, :, :].rearrange("p t g -> p (t g)")
                gb = gsel[:, :, :].rearrange("p t g -> p (t g)")
                dve.tensor_tensor(g, pm[:, :, 0], pm[:, :, 1], ALU.max)
                dve.tensor_tensor(gb, pm[:, :, 0], pm[:, :, 1], ALU.min)
                link(dve.tensor_tensor(pm[:, :, 2], pm[:, :, 2], pm[:, :, 3], ALU.max))
                link(dve.tensor_tensor(gb, gb, pm[:, :, 2], ALU.max))
                link(dve.tensor_tensor(g, g, gb, ALU.add))
                other = gs[:, :, :].rearrange("p t (o g) -> p t o g", o=1).to_broadcast([P, RB, EG, EG])
                own = gs[:, :, :].rearrange("p t (g o) -> p t g o", o=1).to_broadcast([P, RB, EG, EG])
                dve.tensor_tensor(cmp8[:, 0], other, own, ALU.is_gt)
                link(dve.tensor_tensor(cmp8[:, 1], other, own, ALU.is_equal))
                before = con[:, C_GT:C_GT + EG * EG].rearrange("p (o g h) -> p o g h", o=1, g=EG)\
                    .to_broadcast([P, RB, EG, EG])
                link(dve.tensor_tensor(cmp8[:, 1], cmp8[:, 1], before, ALU.mult))
                link(dve.tensor_tensor(cmp8[:, 0], cmp8[:, 0], cmp8[:, 1], ALU.add))
                link(dve.tensor_reduce(gsel[:, :, :], cmp8[:, 0], AXX, ALU.add))
                link(dve.tensor_scalar(gsel[:, :, :], gsel[:, :, :], float(TKG), None, ALU.is_lt))
                link(dve.tensor_tensor(msk[:, :, :].rearrange("p t (g c) -> p (t g) c", c=GSZ),
                                       sb_[:, :, :].rearrange("p t (g c) -> p (t g) c", c=GSZ),
                                       gsel[:, :, :].rearrange("p t (g o) -> p (t g) o", o=1)
                                       .to_broadcast([P, RB * EG, GSZ]), ALU.mult))
                link(dve.tensor_scalar(msk[:, :, :], msk[:, :, :], 0.0, None, ALU.add))
                for t in range(RB):
                    last = dve.max(top[:, t, :], msk[:, t, :])
                link(last)
                for t in range(RB):
                    last = dve.match_replace(rep[:, t, :], top[:, t, :], msk[:, t, :], -3e38)
                link(last)
                dve.tensor_tensor(chosen[:, :, :], rep[:, :, :], msk[:, :, :], ALU.not_equal)\
                    .then_inc(chose, 1)
                dve.wait_ge(chose, r + 1)
                link(dve.tensor_tensor(wn[:, :, :], sc[:, :, :], chosen[:, :, :], ALU.mult))
                link(dve.tensor_reduce(ws[:, :], wn[:, :, :], AXX, ALU.add))
                link(dve.reciprocal(ws[:, :], ws[:, :]))
                link(dve.tensor_tensor(wn[:, :, :], wn[:, :, :],
                                       ws[:, :].rearrange("p (t o) -> p t o", o=1).to_broadcast([P, RB, E]),
                                       ALU.mult))
                link(dve.tensor_scalar(wn[:, :, :], wn[:, :, :], SCALE, None, ALU.mult))

            def assign(r):
                dve.wait_ge(rank_mm, r + 1)
                total = ps1[:, 512:512 + RB * E].rearrange("p (t e) -> p t e", e=E)
                link(dve.tensor_copy(runs[:, 0, :], cnt[:, :]))
                for t in range(RB):
                    link(dve.tensor_tensor(runs[:, t + 1, :], runs[:, t, :], total[:, t, :], ALU.add))
                dve.tensor_copy(cnt[:, :], runs[:, RB, :])
                link(dve.tensor_tensor(key[:, :, :], runs[:, 0:RB, :],
                                       ps1[:, 0:RB * E].rearrange("p (t e) -> p t e", e=E), ALU.add))
                dve.tensor_tensor(key[:, :, :], key[:, :, :],
                                  con[:, C_EB:C_EB + E].rearrange("p (o e) -> p o e", o=1)
                                  .to_broadcast([P, RB, E]), ALU.add).then_inc(rank_used, 1)
                dve.wait_ge(rank_used, r + 2)
                link(dve.scalar_tensor_tensor(out=key[:, :, :], in0=key[:, :, :], scalar=1.0,
                                              in1=chosen[:, :, :], op0=ALU.add, op1=ALU.mult))
                for t in range(RB):
                    last = dve.max(top[:, t, :], key[:, t, :])
                link(last)
                link(dve.tensor_tensor(wide, key[:, :, :].rearrange("p t (o e) -> p t o e", o=1)
                                       .to_broadcast([P, RB, K, E]),
                                       top[:, :, :].rearrange("p t (k o) -> p t k o", o=1)
                                       .to_broadcast([P, RB, K, E]), ALU.is_equal))
                link(dve.tensor_tensor(wide, wide, wn[:, :, :].rearrange("p t (o e) -> p t o e", o=1)
                                       .to_broadcast([P, RB, K, E]), ALU.mult))
                dve.tensor_reduce(wpick[:, bass.ds(r * RB, RB), :], wide, AXX, ALU.add)
                link(dve.tensor_scalar(vslot[:, bass.ds(r * RB, RB), :], top[:, :, :], -1.0, None, ALU.add))
                dve.wait_ge(place_free, r + 1)
                link(dve.tensor_scalar(place[:, :, :], top[:, :, :], -1.0, None, ALU.add))
                link(dve.tensor_copy(toki[:, :], tokf[:, :]))
                dve.tensor_scalar(tokf[:, :], tokf[:, :], float(RB * P), None, ALU.add)\
                    .then_inc(placed, 1)

            dve.sem_inc(rank_used, 1)
            dve.memset(kp[:, 0:P - 1], 0.0).then_inc(kp_zero, 1)
            dve.memset(zero_i, 0).then_inc(kp_zero, 1)
            dve.memset(kp[:, P - 1 + L:P + L], 0.0)
            dve.memset(cnt[:, :], 0.0)
            dve.wait_ge(setup_ld, 80)
            link(dve.tensor_copy(tokf[:, :], con[:, C_TOK:C_TOK + RB]))
            dve.tensor_tensor(kp[:, P - 1:P], kp[:, P - 1:P], sd_in[0:HEADS, 0:1], ALU.add)\
                .then_inc(kp_ready, 1)
            dve.wait_ge(kp_ready, 1)
            dve.wait_ge(kpad_st, 16)
            dve.wait_ge(lists_st, 32)
            walk(dve, step, seq)
            assign(NTILE // RB - 1)

        @block.tensor
        def _(pe):
            def free0(s, toep_now=0, xin_now=0):
                wait(pe, toep_copied, s.past(TOEP) + toep_now)
                wait(pe, xin_copied, s.past(INS) + xin_now)
                wait(pe, x2T_copied, s.past(ROUTE))

            def free1(s, out_now=0, ctx_now=0, routed=0):
                wait(pe, out_added, s.past(OUT) + out_now)
                wait(pe, ctx_copied, s.past(INS) + ctx_now)
                wait(pe, lg_copied, s.past(ROUTE) + routed)
                done = s.block - 2 + (s.u > 2)
                pe.wait_ge(rank_used, 1 + (done if not isinstance(s.block, int) else max(done, 0)))

            def conv(s, lb):
                if not s.on(CONV):
                    return
                n, sl = s.n(CONV), s.slot(CONV)
                if lb == 0:
                    pe.wait_ge(kv_built, n + 1)
                    pe.wait_ge(toep_copied, n + 1)
                m = 8 * n + lb
                wait(pe, y_copied, max(m - 1, 0) if isinstance(m, int) else m - 1)
                for d in range(lb + 1):
                    for half in range(2):
                        row = (lb - d) * B + half * B // 2
                        last = pe.matmul(yps[lb % 2][:, half, 0:NH], toep[sl][:, d * P:(d + 1) * P],
                                         kv[sl][:, row:row + B // 2, :],
                                         start=(d == 0), stop=(d == lb))
                last.then_inc(y_mm, 1)
                if lb == LB - 1:
                    pe.nop().then_inc(conv_done, 1)

            def step(s):
                if s.on(TOEP):
                    pe.wait_ge(t_ld[s.slot(TOEP)], 16 * (s.half(TOEP) + 1))
                    free0(s)
                    for i in range(2):
                        last = pe.matmul(ps0[:, i * 512:(i + 1) * 512], con[:, C_REV:C_REV + P],
                                         traw[s.slot(TOEP)][:, i * 512:(i + 1) * 512], start=True, stop=True)
                    last.then_inc(toep_mm, 1)
                for lb in range(5):
                    conv(s, lb)
                if s.on(OUT):
                    pe.wait_ge(second_half, HPG * (s.group(OUT) + 1))
                    free1(s)
                    o = qT[s.gslot(OUT)][:, :, :].rearrange("p (m q b) c -> p m q (b c)", m=LB, b=BT)
                    for m in range(LB):
                        last = pe.transpose(ps1[:, m * P:(m + 1) * P], o[:, m, s.quarter(OUT)], ident)
                    last.then_inc(out_mm, 1)
                if s.on(INS):
                    pe.wait_ge(normed, s.n(INS) + 1)
                    free0(s, toep_now=int(s.on(TOEP)))
                    for m in range(LB):
                        last = pe.transpose(ps0[:, m * P:(m + 1) * P],
                                            xin[s.slot(INS)][:, m * P:(m + 1) * P], ident)
                    last.then_inc(xin_mm, 1)
                conv(s, 5)
                if s.on(INS):
                    pe.wait_ge(c_ld[s.slot(INS)], 16 * (s.half(INS) + 1))
                    free1(s, out_now=int(s.on(OUT)))
                    for m in range(LB):
                        last = pe.transpose(ps1[:, m * P:(m + 1) * P],
                                            cin[s.slot(INS)][:, m * P:(m + 1) * P], ident)
                    last.then_inc(ctx_mm, 1)
                if s.on(ROUTE):
                    pe.wait_ge(normed2, s.n(ROUTE) + 1)
                    free0(s, toep_now=int(s.on(TOEP)), xin_now=int(s.on(INS)))
                    for m in range(LB):
                        last = pe.transpose(ps0[:, m * P:(m + 1) * P],
                                            xn2[s.slot(ROUTE)][:, m * P:(m + 1) * P], ident)
                    last.then_inc(x2T_mm, 1)
                conv(s, 6)
                if s.on(ROUTE):
                    pe.wait_ge(x2T_copied, s.n(ROUTE) + 1)
                    free1(s, out_now=int(s.on(OUT)), ctx_now=int(s.on(INS)))
                    for m in range(LB):
                        last = pe.matmul(ps1[:, 0:E], x2T[:, m, :], rws[:, m, :],
                                         start=(m == 0), stop=(m == LB - 1))
                    last.then_inc(lg_mm, 1)
                conv(s, 7)
                if routes(s, 2):
                    ranks(s, s.block - 2)

            def ranks(s, r):
                pe.wait_ge(chose, r + 1)
                wait(pe, out_added, s.past(OUT) + int(s.on(OUT)))
                wait(pe, ctx_copied, s.past(INS) + int(s.on(INS)))
                wait(pe, lg_copied, s.past(ROUTE) + int(s.on(ROUTE)))
                m = chosen[:, :, :].rearrange("p t e -> p (t e)")
                pe.matmul(ps1[:, 0:RB * E], con[:, C_TRI:C_TRI + P], m, start=True, stop=True)
                pe.matmul(ps1[:, 512:512 + RB * E], con[:, C_ONE:C_ONE + P], m, start=True, stop=True)\
                    .then_inc(rank_mm, 1)

            pe.wait_ge(setup_ld, 80)
            walk(pe, step)
            ranks(Step(BLOCKS, 0), NTILE // RB - 1)


def routes(s, u):
    return s.u == u and (not isinstance(s.block, int) or 2 <= s.block)


def plan(nc, A, keep):
    es = ExitStack()
    with es:
        def sb(name, shape, dt=F32):
            return es.enter_context(nc.sbuf_tensor(name, shape, dt))

        con, vslot, cnt, pick, table = (keep[k] for k in ("con", "vslot", "cnt", "pick", "table"))
        orow = keep["orow"]
        fields = sb("fields", [P, TCOLS * P, FIELDS], I32)
        over = sb("over", [P, EXPERT_TILES])
        rows = sb("rows", [P, EXPERT_TILES])
        nti = sb("nti", [P, E], I32)
        nt = sb("nt", [P, NE])
        tend = sb("tend", [P, NE])
        shift = sb("shift", [P, E])
        spot = sb("spot", [P, NTILE * K])
        part = sb("part", [P, NTILE * K])
        past = sb("past", [P, TCOLS, NE - 1])
        pastn = sb("pastn", [P, TCOLS, NE - 1])
        ex = sb("ex", [P, TCOLS])
        at = sb("at", [P, TCOLS])
        rowf = sb("rowf", [P, TCOLS])
        start = sb("start", [P, TCOLS])
        end = sb("end", [P, TCOLS])
        tab = sb("tab", [P, TCOLS, FIELDS], I32)
        seq_sem = es.enter_context(nc.semaphore("plan_seq"))
        tab_ready = es.enter_context(nc.semaphore("tab_ready"))
        tab_st = es.enter_context(nc.semaphore("tab_st"))
        tab_ld = es.enter_context(nc.semaphore("tab_ld"))
        block = es.enter_context(nc.Block())

        @block.sync
        def _(sp):
            sp.wait_ge(tab_ready, 1)
            sp.dma_start(A["tabd"].rearrange("(c p k) -> p c k", p=P, k=FIELDS), tab[:, :, :])\
                .then_inc(tab_st, 16)
            sp.wait_ge(tab_st, 16)
            sp.dma_start(table[:, :], A["tabd"].rearrange("(o n) -> o n", o=1)).then_inc(tab_ld, 16)
            sp.dma_start(fields[:, :, :].rearrange("p t k -> p (t k)"),
                         A["tabd"].rearrange("(o n) -> o n", o=1).to_broadcast([P, TCOLS * P * FIELDS]))\
                .then_inc(tab_ld, 16)
            sp.wait_ge(tab_ld, 32)

        @block.vector
        def _(dve):
            seq = Chain(seq_sem)

            def link(ins):
                seq.link(dve, ins)

            link(dve.tensor_scalar(nti[:, :], cnt[:, :], float(P - 1), None, ALU.add))
            link(dve.tensor_scalar(nti[:, :], nti[:, :], P.bit_length() - 1, None, ALU.logical_shift_right))
            link(dve.tensor_scalar(nt[:, 0:E], nti[:, :], 1.0, None, ALU.max))
            link(dve.tensor_tensor_scan(tend[:, 0:E], con[:, C_ONE:C_ONE + E], nt[:, 0:E], 0.0,
                                        ALU.mult, ALU.add))
            link(dve.tensor_scalar(shift[:, :], cnt[:, :], float(-LIST), None, ALU.add))
            link(dve.tensor_scalar(nt[:, E - 1:E], tend[:, E - 2:E - 1], -1.0, float(SH0), ALU.mult, ALU.add))
            dve.memset(nt[:, E:E + 1], float(NTILE))
            dve.memset(tend[:, E - 1:E], float(SH0))
            link(dve.memset(tend[:, E:E + 1], float(SH1)))
            tn = con[:, C_T:C_T + TCOLS].rearrange("p (c o) -> p c o", o=1).to_broadcast([P, TCOLS, NE - 1])
            ends = tend[:, 0:NE - 1].rearrange("p (o e) -> p o e", o=1).to_broadcast([P, TCOLS, NE - 1])
            nts = nt[:, 0:NE - 1].rearrange("p (o e) -> p o e", o=1).to_broadcast([P, TCOLS, NE - 1])
            link(dve.tensor_tensor(past[:, :, :], tn, ends, ALU.is_ge))
            dve.tensor_reduce(ex[:, :], past[:, :, :], AXX, ALU.add)
            link(dve.tensor_tensor(pastn[:, :, :], past[:, :, :], nts, ALU.mult))
            link(dve.tensor_reduce(at[:, :], pastn[:, :, :], AXX, ALU.add))

            def tokens_of(first):
                c = cnt[:, first:first + E - 1].rearrange("p (o e) -> p o e", o=1).to_broadcast([P, TCOLS, E - 1])
                return dve.tensor_tensor(pastn[:, :, 0:E - 1], past[:, :, 0:E - 1], c, ALU.mult)

            link(tokens_of(0))
            link(dve.tensor_reduce(start[:, :], pastn[:, :, 0:E - 1], AXX, ALU.add))
            link(tokens_of(1))
            link(dve.tensor_reduce(end[:, :], pastn[:, :, 0:E - 1], AXX, ALU.add))
            link(dve.tensor_scalar(tab[:, :, F_END], end[:, :], cnt[:, 0:1], None, ALU.add))
            link(dve.tensor_tensor(at[:, :], con[:, C_T:C_T + TCOLS], at[:, :], ALU.subtract))
            link(dve.scalar_tensor_tensor(out=tab[:, :, F_START], in0=at[:, :], scalar=float(P),
                                          in1=start[:, :], op0=ALU.mult, op1=ALU.add))
            link(dve.tensor_scalar(at[:, :], at[:, :], float(LROWS - 1), None, ALU.min))
            link(dve.tensor_scalar(rowf[:, :], ex[:, :], float(E), float(LROWS), ALU.min, ALU.mult))
            dve.tensor_copy(tab[:, :, F_EXPERT], ex[:, :])
            dve.tensor_scalar(tab[:, :, F_FIRST], at[:, :], 0.0, None, ALU.is_equal)
            dve.tensor_tensor(tab[:, :, F_ROW], rowf[:, :], at[:, :], ALU.add).then_inc(tab_ready, 1)
            v = vslot[:, :, :].rearrange("p t k -> p (t k)")
            link(dve.tensor_copy(spot[:, :], v))
            for e in range(1, E):
                link(dve.tensor_scalar(part[:, :], v, float(LIST * e), shift[:, e - 1:e], ALU.is_ge, ALU.mult))
                link(dve.tensor_tensor(spot[:, :], spot[:, :], part[:, :], ALU.add))
            link(dve.tensor_copy(pick[:, :, :].rearrange("p t k -> p (t k)"), spot[:, :]))
            dve.wait_ge(tab_ld, 32)
            f = fields[:, 0:EXPERT_TILES, :]
            link(dve.tensor_scalar(rows[:, :], f[:, :, F_START], con[:, C_T:C_T + 1], None, ALU.add))
            link(dve.tensor_tensor(over[:, :], rows[:, :], f[:, :, F_END], ALU.is_ge))
            link(dve.scalar_tensor_tensor(out=orow[:, :], in0=over[:, :], scalar=float(2 * NTOK * K),
                                          in1=rows[:, :], op0=ALU.mult, op1=ALU.add))


class Tile:

    def __init__(self, first, u=0, turn=0, shared=False, sums=False):
        self.first, self.u, self.turn, self.fixed = first, u, turn, isinstance(turn, int)
        self.shared, self.sums = shared, sums

    def n(self, k=0):
        return self.first + self.u + k + 2 * self.turn

    def slot(self, k=0):
        return (self.first + self.u + k) % 2

    def half(self, k=0):
        return (self.first + self.u + k) // 2 + self.turn

    def on(self, k=0):
        return not self.fixed or 0 <= self.n(k) < TILES


PEELED = 3
ROUTED_TURNS = (SH0 + 1 - PEELED) // 2
SHARED_TURNS = NTILE // 2
SUM_TURNS = NTILE // 2 - 3


def walk_tiles(eng, tile, before_sums=None):
    for t in range(PEELED):
        tile(Tile(t))
    with eng.Fori(0, ROUTED_TURNS) as turn:
        for u in range(2):
            tile(Tile(PEELED, u, turn))
    with eng.Fori(0, SHARED_TURNS) as turn:
        for u in range(2):
            tile(Tile(SH0 + 1, u, turn, shared=True))
    if before_sums:
        before_sums()
    tile(Tile(SH1 + 1, sums=True))
    with eng.Fori(0, SUM_TURNS) as turn:
        for u in range(2):
            tile(Tile(SH1 + 2, u, turn, sums=True))
    for t in range(SH1 + 2 + 2 * SUM_TURNS, TILES + 1):
        tile(Tile(t, sums=True))


def feed_forward(nc, A, keep):
    xnd, x2d, lists, yd, out = A["xnd"], A["x2d"], A["lists"], A["yd"], A["out"]
    shd = A["shd"]
    es = ExitStack()
    with es:
        def sb(name, shape, dt=F32):
            return es.enter_context(nc.sbuf_tensor(name, shape, dt))

        def sem(name):
            return es.enter_context(nc.semaphore(name))

        con, wpick, pick, table = (keep[k] for k in ("con", "wpick", "pick", "table"))
        orow = keep["orow"]
        ident = con[:, C_ID:C_ID + P]
        KX, KH = L // P, I // P
        whi = sb("whi", [P, KX + KH, 2 * I], F32R)
        wlo = sb("wlo", [P, KX + KH, 2 * I], F32R)
        raw = sb("raw", [P, KX + KH, 2 * I])
        idx = [sb(f"idx{i}", [P, 1], I32) for i in range(2)]
        gidx = [sb(f"gidx{i}", [P, K], I32) for i in range(2)]
        yidx = [sb(f"yidx{i}", [P, 1], I32) for i in range(2)]
        xg = [sb(f"xg{i}", [P, L]) for i in range(2)]
        xhi, xlo = sb("xhi", [P, KX, P], F32R), sb("xlo", [P, KX, P], F32R)
        sg, hb = sb("sg", [P, I]), sb("hb", [P, I])
        hhi, hlo = sb("hhi", [P, KH, P], F32R), sb("hlo", [P, KH, P], F32R)
        ysb = [sb(f"ysb{i}", [P, L]) for i in range(2)]
        picked = [raw[:, k, :] for k in range(K)]
        acc = [raw[:, K + i, :] for i in range(2)]
        ysh = [raw[:, K + 2 + i, :] for i in range(2)]

        gps = es.enter_context(nc.psum_tensor("gps", [P, 512], F32))
        ups = es.enter_context(nc.psum_tensor("ups", [P, 512], F32))
        xps = es.enter_context(nc.psum_tensor("xps", [P, 1024], F32))
        hps = es.enter_context(nc.psum_tensor("hps", [P, 512], F32))
        yps = es.enter_context(nc.psum_tensor("yps", [P, 1024], F32))

        w_ld = [sem(f"w_ld{q}") for q in range(UNITS)]
        hi_gu, lo_gu, hi_dn, lo_dn = sem("hi_gu"), sem("lo_gu"), sem("hi_dn"), sem("lo_dn")
        idx_ld = [sem(f"idx_ld{i}") for i in range(2)]
        x_ld = [sem(f"xg_ld{i}") for i in range(2)]
        y_st = [sem(f"y_st{i}") for i in range(2)]
        out_st = [sem(f"out_st{i}") for i in range(2)]
        acc_ld = [sem(f"acc_ld{i}") for i in range(2)]
        ysh_ld = [sem(f"ysh_ld{i}") for i in range(2)]
        pick_ld = [sem(f"pick_ld{k}") for k in range(K)]
        pool_turns = sem("pool_turns2")
        gidx_ready, yidx_ready = sem("gidx_ready"), sem("yidx_ready")
        gu_mm, xT_mm, down_mm, hT_mm = sem("gu_mm"), sem("xT_mm"), sem("down_mm"), sem("hT_mm")
        silu_done, h_done = sem("silu_done"), sem("h_done")
        x_hi, x_lo, h_hi, h_lo = sem("x_hi"), sem("x_lo"), sem("h_hi"), sem("h_lo")
        y_act, y_dve, pick_used, ysh_used = sem("y_act"), sem("y_dve"), sem("pick_used"), sem("ysh_used")
        block = es.enter_context(nc.Block())

        def entry(eng, t, what, most):
            return eng.value_load(table[0:1, bass.ds(t * FIELDS + what, 1)], min_val=0, max_val=most)

        def expert(eng, t):
            return 0 if isinstance(t, int) and t == 0 else entry(eng, t, F_EXPERT, NE - 1)

        @block.sync
        def _(sp):
            def load(e, gate, up, down):
                for q in range(GU):
                    wait(sp, lo_gu, GU * (e - 1) + q + 1 if not (isinstance(e, int) and e == 0) else 0)
                    for src, c in ((gate, 0), (up, I)):
                        sp.dma_start(raw[:, 2 * q:2 * q + 2, c:c + I],
                                     src[2 * q * P:(2 * q + 2) * P, :].rearrange("(k p) i -> p k i", p=P))\
                            .then_inc(w_ld[q], 16)
                for q in range(DN):
                    wait(sp, lo_dn, DN * (e - 1) + q + 1 if not (isinstance(e, int) and e == 0) else 0)
                    sp.dma_start(raw[:, KX + 2 * q:KX + 2 * q + 2, :],
                                 down[2 * q * P:(2 * q + 2) * P, :].rearrange("(k p) i -> p k i", p=P))\
                        .then_inc(w_ld[GU + q], 16)

            def routed(e):
                one = slice(e, e + 1) if isinstance(e, int) else bass.ds(e, 1)
                load(e, *(A[k][one].rearrange("o a b -> (o a) b") for k in ("w_gate", "w_up", "w_down")))

            routed(0)
            with sp.Fori(0, E - 1) as turn:
                routed(turn + 1)
            for s in range(NE - E):
                cols = slice(s * I, (s + 1) * I)
                load(E + s, A["sw_gate"][:, cols], A["sw_up"][:, cols], A["sw_down"][cols, :])

            sp.wait_ge(lo_dn, DN * NE)
            sp.wait_ge(y_st[0], 16 * SH1 // 2)
            sp.wait_ge(y_st[1], 16 * SH1 // 2)

            def fetch(half, i):
                n = 2 * half + i
                wait(sp, out_st[i], 16 * BT * half)
                sp.dma_start(acc[i], x2d[bass.ds(n * P, P), :]).then_inc(acc_ld[i], 16)
                wait(sp, ysh_used, n - 1 if not isinstance(n, int) else max(n - 1, 0))
                sp.dma_start(ysh[i], shd[bass.ds(n * P, P), :]).then_inc(ysh_ld[i], 16)

            for i in range(2):
                fetch(0, i)
            with sp.Fori(0, NTILE // 2 - 1) as turn:
                for i in range(2):
                    fetch(turn + 1, i)

        @block.gpsimd
        def _(pool):
            def load_list(t, slot, turns):
                row = entry(pool, t, F_ROW, (E + 1) * LROWS - 1)
                wait(pool, x_ld[slot], 16 * turns)
                pool.dma_start(idx[slot][:, :], lists[bass.ds(row * P, P), :]).then_inc(idx_ld[slot], 16)

            def gather(t, slot, turns):
                wait(pool, xT_mm, t - 1 if not isinstance(t, int) else max(t - 1, 0))
                pool.wait_ge(idx_ld[slot], 16 * (turns + 1))
                settle(pool, pool_turns)
                pool.indirect_dma_start(out=xg[slot][:, :], out_offset=None, in_=xnd,
                                        in_offset=bass.IndirectOffsetOnAxis(ap=idx[slot][:, 0:1], axis=0))\
                    .then_inc(x_ld[slot], 16)

            def fetch_picks(n, slot):
                wait(pool, pick_used, K * (n - 1) if not isinstance(n, int) else max(K * (n - 1), 0))
                pool.tensor_copy(gidx[slot][:, :], pick[:, bass.ds(n, 1), :].rearrange("p o k -> p (o k)"))\
                    .then_inc(gidx_ready, 1)
                pool.wait_ge(gidx_ready, n + 1)
                for k in range(K):
                    if not isinstance(n, int) or n > 0:
                        pool.wait_ge(pick_used, K * (n - 1) + k + 1)
                    settle(pool, pool_turns)
                    pool.indirect_dma_start(out=picked[k], out_offset=None, in_=yd,
                                            in_offset=bass.IndirectOffsetOnAxis(ap=gidx[slot][:, k:k + 1], axis=0))\
                        .then_inc(pick_ld[k], 16)

            def tile(c):
                if c.on(3):
                    load_list(c.n(3), c.slot(3), c.half(3))
                if c.on(2):
                    gather(c.n(2), c.slot(2), c.half(2))
                if c.sums:
                    n = c.n(-SH1)
                    if not c.fixed or n < NTILE:
                        fetch_picks(n, c.slot(-SH1))
                elif c.on(-1):
                    store(c, c.slot(-1))

            def store(c, i):
                if not c.shared:
                    wait(pool, y_st[i], 16 * c.half(-1))
                    pool.tensor_copy(yidx[i][:, :], orow[:, bass.ds(c.n(-1), 1)]).then_inc(yidx_ready, 1)
                    pool.wait_ge(yidx_ready, c.n())
                pool.wait_ge(y_act, c.n())
                pool.wait_ge(y_dve, c.n())
                settle(pool, pool_turns)
                if c.shared:
                    pool.dma_start(shd[bass.ds((c.n(-1) - SH0) * P, P), :], ysb[i][:, :]).then_inc(y_st[i], 16)
                else:
                    pool.indirect_dma_start(out=yd, in_=ysb[i][:, :], in_offset=None,
                                            out_offset=bass.IndirectOffsetOnAxis(ap=yidx[i][:, 0:1], axis=0),
                                            bounds_check=NTOK * K - 1, oob_is_err=False).then_inc(y_st[i], 16)

            def before_sums():
                pool.wait_ge(lo_dn, DN * NE)
                pool.wait_ge(y_st[0], 16 * SH1 // 2)
                pool.wait_ge(y_st[1], 16 * SH1 // 2)
                fetch_picks(0, 0)

            for t in range(3):
                if t == 2:
                    gather(0, 0, 0)
                    gather(1, 1, 0)
                load_list(t, t % 2, t // 2)
            walk_tiles(pool, tile, before_sums)

        @block.scalar
        def _(act):
            def split_gu(e):
                for q in range(GU):
                    act.wait_ge(w_ld[q], 32 * (e + 1))
                    act.activation(whi[:, 2 * q:2 * q + 2, :], raw[:, 2 * q:2 * q + 2, :], ACT.Copy)\
                        .then_inc(hi_gu, 1)

            def split_dn(e):
                for q in range(DN):
                    act.wait_ge(w_ld[GU + q], 16 * (e + 1))
                    act.activation(whi[:, KX + 2 * q:KX + 2 * q + 2, :], raw[:, KX + 2 * q:KX + 2 * q + 2, :],
                                   ACT.Copy).then_inc(hi_dn, 1)

            def x_high(t):
                act.wait_ge(xT_mm, t + 1)
                act.activation(xhi[:, :, :].rearrange("p k t -> p (k t)"), xps[:, :], ACT.Copy).then_inc(x_hi, 1)

            def tile(c):
                t = c.n()
                if c.on():
                    act.wait_ge(gu_mm, t + 1)
                    act.activation(sg[:, :], gps[:, :], ACT.Silu).then_inc(silu_done, 1)
                if c.on(1):
                    x_high(c.n(1))
                    if not c.sums:
                        with act.If(entry(act, c.n(1), F_FIRST, 1) == 1):
                            split_gu(entry(act, c.n(1), F_EXPERT, NE - 1))
                if c.on(-1) and not c.sums:
                    act.wait_ge(down_mm, t)
                    wait(act, y_st[c.slot(-1)], 16 * c.half(-1))
                    act.activation(ysb[c.slot(-1)][:, 0:512], yps[:, 0:512], ACT.Copy).then_inc(y_act, 1)
                if c.on():
                    act.wait_ge(hT_mm, t + 1)
                    act.activation(hhi[:, :, :].rearrange("p k t -> p (k t)"), hps[:, :], ACT.Copy).then_inc(h_hi, 1)
                if c.fixed and t == 0:
                    split_dn(0)
                elif not c.sums:
                    with act.If(entry(act, t, F_FIRST, 1) == 1):
                        e = entry(act, t, F_EXPERT, NE - 1)
                        act.wait_ge(down_mm, t)
                        split_dn(e)
                if c.sums:
                    store_sum(c)

            def store_sum(c):
                if c.fixed and c.n(-2 - SH1) < 0:
                    return
                n, i = c.n(-2 - SH1), c.slot(-2 - SH1)
                act.wait_ge(y_dve, c.n(-1))
                for b in range(BT):
                    dst = out[bass.ds(n % TPG * BT + b, 1), bass.ds(n // TPG * CG, CG), :]
                    act.dma_start(dst.rearrange("o c l -> (o c) l"), acc[i][b * CG:(b + 1) * CG, :])\
                        .then_inc(out_st[i], 16)

            split_gu(0)
            x_high(0)
            walk_tiles(act, tile)
            store_sum(Tile(TILES + 1, sums=True))
            for i in range(2):
                act.wait_ge(out_st[i], 16 * BT * NTILE // 2)

        @block.vector
        def _(dve):
            def low(dst, src, hi):
                return dve.tensor_tensor(dst, src, hi.bitcast(F32), ALU.subtract)

            def split_gu(e):
                for q in range(GU):
                    r = slice(2 * q, 2 * q + 2)
                    dve.wait_ge(hi_gu, GU * e + q + 1)
                    low(wlo[:, r, :], raw[:, r, :], whi[:, r, :]).then_inc(lo_gu, 1)

            def split_dn(e):
                for q in range(DN):
                    r = slice(KX + 2 * q, KX + 2 * q + 2)
                    dve.wait_ge(hi_dn, DN * e + q + 1)
                    low(wlo[:, r, :], raw[:, r, :], whi[:, r, :]).then_inc(lo_dn, 1)

            def x_low(t):
                dve.wait_ge(x_hi, t + 1)
                low(xlo[:, :, :].rearrange("p k t -> p (k t)"), xps[:, :],
                    xhi[:, :, :].rearrange("p k t -> p (k t)")).then_inc(x_lo, 1)

            def add_picks(n, i, half):
                dve.wait_ge(acc_ld[i], 16 * (half + 1))
                for k in range(K):
                    dve.wait_ge(pick_ld[k], 16 * (n + 1))
                    dve.scalar_tensor_tensor(
                        out=acc[i], in0=picked[k],
                        scalar=wpick[:, bass.ds(n, 1), k:k + 1].rearrange("p o k -> p (o k)"),
                        in1=acc[i], op0=ALU.mult, op1=ALU.add).then_inc(pick_used, 1)
                    dve.wait_ge(pick_used, K * n + k + 1)
                dve.wait_ge(ysh_ld[i], 16 * (half + 1))
                dve.tensor_tensor(acc[i], acc[i], ysh[i], ALU.add).then_inc(ysh_used, 1)
                dve.wait_ge(ysh_used, n + 1)

            def tile(c):
                t = c.n()
                if c.on():
                    dve.wait_ge(silu_done, t + 1)
                    wait(dve, hT_mm, t)
                    dve.tensor_tensor(hb[:, :], sg[:, :], ups[:, :], ALU.mult).then_inc(h_done, 1)
                if c.on(1):
                    x_low(c.n(1))
                    if not c.sums:
                        with dve.If(entry(dve, c.n(1), F_FIRST, 1) == 1):
                            split_gu(entry(dve, c.n(1), F_EXPERT, NE - 1))
                if c.sums:
                    n, i = c.n(-1 - SH1), c.slot(-1 - SH1)
                    add_picks(n, i, c.half(-1 - SH1))
                    dve.wait_ge(down_mm, t)
                    dve.tensor_tensor(acc[i], acc[i], yps[:, :], ALU.add).then_inc(y_dve, 1)
                elif c.on(-1):
                    dve.wait_ge(down_mm, t)
                    wait(dve, y_st[c.slot(-1)], 16 * c.half(-1))
                    dve.tensor_copy(ysb[c.slot(-1)][:, 512:1024], yps[:, 512:1024]).then_inc(y_dve, 1)
                if c.on():
                    dve.wait_ge(h_hi, t + 1)
                    low(hlo[:, :, :].rearrange("p k t -> p (k t)"), hps[:, :],
                        hhi[:, :, :].rearrange("p k t -> p (k t)")).then_inc(h_lo, 1)
                if c.fixed and t == 0:
                    split_dn(0)
                elif not c.sums:
                    with dve.If(entry(dve, t, F_FIRST, 1) == 1):
                        split_dn(entry(dve, t, F_EXPERT, NE - 1))

            split_gu(0)
            x_low(0)
            walk_tiles(dve, tile)

        @block.tensor
        def _(pe):
            def three(hi, lo, chunk, outs, first, last_one):
                passes = ((hi, whi), (hi, wlo), (lo, whi))
                for n, (rows, w) in enumerate(passes):
                    for i, ps in enumerate(outs):
                        ins = pe.matmul(ps, rows, w[:, chunk, i * 512:(i + 1) * 512],
                                        start=first and n == 0, stop=last_one and n == 2)
                return ins

            def transpose_rows(t, slot, turns):
                pe.wait_ge(x_ld[slot], 16 * (turns + 1))
                for m in range(KX):
                    last = pe.transpose(xps[:, m * P:(m + 1) * P], xg[slot][:, m * P:(m + 1) * P], ident)
                last.then_inc(xT_mm, 1)

            def tile(c):
                t = c.n()
                if c.on():
                    e = expert(pe, t)
                    pe.wait_ge(x_lo, t + 1)
                    wait(pe, h_done, t)
                    for m in range(KX):
                        if m % 2 == 0:
                            pe.wait_ge(lo_gu, GU * e + m // 2 + 1)
                        last = three(xhi[:, m, :], xlo[:, m, :], m, (gps[:, :], ups[:, :]),
                                     m == 0, m == KX - 1)
                    last.then_inc(gu_mm, 1)
                if c.on(1):
                    transpose_rows(c.n(1), c.slot(1), c.half(1))
                if c.on(-1):
                    e = expert(pe, c.n(-1))
                    pe.wait_ge(h_lo, t)
                    if c.sums:
                        wait(pe, y_act, SH1)
                    else:
                        wait(pe, y_act, c.n(-1))
                    wait(pe, y_dve, c.n(-1))
                    for m in range(KH):
                        if m % 2 == 0:
                            pe.wait_ge(lo_dn, DN * e + m // 2 + 1)
                        last = three(hhi[:, m, :], hlo[:, m, :], KX + m,
                                     (yps[:, 0:512], yps[:, 512:1024]), m == 0, m == KH - 1)
                    last.then_inc(down_mm, 1)
                if c.on():
                    pe.wait_ge(h_done, t + 1)
                    for m in range(KH):
                        last = pe.transpose(hps[:, m * P:(m + 1) * P], hb[:, m * P:(m + 1) * P], ident)
                    last.then_inc(hT_mm, 1)

            transpose_rows(0, 0, 0)
            walk_tiles(pe, tile)


def program(nc, x, ctx, kern, dvec, rw, bias, w_gate, w_up, w_down, sw_gate, sw_up, sw_down,
            con_d, tokens, out):
    A = dict(x=x, ctx=ctx, kern=kern, dvec=dvec, rw=rw, bias=bias, w_gate=w_gate, w_up=w_up,
             w_down=w_down, sw_gate=sw_gate, sw_up=sw_up, sw_down=sw_down, con=con_d, tokens=tokens, out=out)
    A["kpad"] = nc.dram_tensor("kpad", (HEADS, L + P), F32).ap()
    A["x2d"] = nc.dram_tensor("x2d", (NTOK, L), F32).ap()
    A["xnd"] = nc.dram_tensor("xnd", (NTOK, L), F32).ap()
    A["lists"] = nc.dram_tensor("lists", ((E + 1) * LIST, 1), I32).ap()
    A["yd"] = nc.dram_tensor("yd", (NTOK * K, L), F32).ap()
    A["shd"] = nc.dram_tensor("shd", (NTOK, L), F32).ap()
    A["tabd"] = nc.dram_tensor("tabd", (TCOLS * P * FIELDS,), I32).ap()
    with ExitStack() as es:
        def sb(name, shape, dt=F32):
            return es.enter_context(nc.sbuf_tensor(name, shape, dt))
        keep = dict(con=sb("con_sb", [P, C_N]), vslot=sb("vslot", [P, NTILE, K]),
                    wpick=sb("wpick", [P, NTILE, K]), cnt=sb("cnt", [P, E]))
        mix_and_route(nc, A, keep)
        keep["pick"] = sb("pick", [P, NTILE, K], I32)
        keep["table"] = sb("table", [1, TCOLS * P * FIELDS], I32)
        keep["orow"] = sb("orow", [P, EXPERT_TILES], I32)
        plan(nc, A, keep)
        feed_forward(nc, A, keep)


_INS = ["x", "ctx_2048", "L0_xattn_ssm_kernel", "L0_xattn_D", "L0_ffn_router_w", "L0_ffn_router_bias",
        "L0_ffn_w_gate", "L0_ffn_w_up", "L0_ffn_w_down", "L0_ffn_sw_gate", "L0_ffn_sw_up", "L0_ffn_sw_down"]


def kernel(**inputs):
    import numpy as _np
    import concourse.bacc as _bacc
    from concourse.bass_utils import run_bass_kernel_spmd as _run

    nc = _bacc.Bacc("TRN2", target_bir_lowering=False, num_devices=1)
    con, tokens = constants()
    arrays, args = {}, []
    for name, a in [(n, inputs[n]) for n in _INS] + [("con", con), ("tokens", tokens)]:
        a = _np.ascontiguousarray(a)
        arrays[f"in_{name}_dram"] = a
        args.append(nc.dram_tensor(f"in_{name}_dram", a.shape, mybir.dt.from_np(a.dtype),
                                   kind="ExternalInput").ap())
    args.append(nc.dram_tensor("out_dram", (B, CH, L), F32, kind="ExternalOutput").ap())
    program(nc, *args)
    return _run(nc, [arrays], core_ids=[0]).results[0]["out_dram"]
```

```python
import concourse.bass as bass
from concourse import mybir
from contextlib import ExitStack

F32 = mybir.dt.float32
F32R = mybir.dt.float32r
I32 = mybir.dt.int32
ALU = mybir.AluOpType
ACT = mybir.ActivationFunctionType
AXX = mybir.AxisListType.X

P = 128
B, CH, L = 16, 512, 1024
HD = 8
HEADS = CH // HD
PAIRS = HD * (HD + 1) // 2
LB = L // P
CG = 32
HPG = CG // HD
BT = P // CG
TPG = B // BT
NTOK = B * CH
NTILE = NTOK // P
HB = B // 2
NH = HB * PAIRS
EPS = 1e-5

E, EG, GSZ, TKG, K = 32, 8, 4, 4, 8
I, SI = 512, 1024
SCALE = 2.5
RB = 8
LIST = NTOK
LROWS = LIST // P
EXPERT_TILES = NTOK * K // P + E
SH0 = EXPERT_TILES
SH1 = SH0 + NTILE
TILES = SH1 + NTILE
TCOLS = -(-TILES // P)
NE = E + SI // I
GU, DN = 4, 2
UNITS = GU + DN

C_ID, C_REV, C_TRI, C_ONE = 0, 128, 256, 384
C_GT = 512
C_EB = C_GT + EG * EG
C_TOK = C_EB + E
C_T = C_TOK + RB
C_EPS = C_T + TCOLS
C_N = C_EPS + 1

F_EXPERT, F_FIRST, F_ROW = range(3)
F_START, F_END = range(2)
FIELDS, OFIELDS = 3, 2


def constants():
    import numpy as np
    c = np.zeros((P, C_N), np.float32)
    p = np.arange(P)
    c[p, C_ID + p] = 1
    c[p, C_REV + P - 1 - p] = 1
    c[:, C_TRI:C_TRI + P] = p[:, None] < p[None, :]
    c[:, C_ONE:C_ONE + P] = 1
    g = np.arange(EG)
    c[:, C_GT:C_GT + EG * EG] = (g[None, :] < g[:, None]).reshape(1, -1)
    c[:, C_EB:C_EB + E] = LIST * np.arange(E)
    c[:, C_TOK:C_TOK + RB] = p[:, None] + P * np.arange(RB)
    c[:, C_T:C_T + TCOLS] = p[:, None] + P * np.arange(TCOLS)
    c[:, C_EPS] = EPS
    return c, np.arange(NTOK, dtype=np.int32).reshape(NTOK, 1)


class Chain:

    def __init__(self, sem):
        self.sem, self.n = sem, 0

    def link(self, eng, ins):
        ins.then_inc(self.sem, 1)
        self.n += 1
        eng.wait_ge(self.sem, self.n)

    def restart(self, eng):
        eng.sem_clear(self.sem)
        self.n = 0


class Step:

    def __init__(self, block, u):
        self.block, self.u = block, u

    def n(self, k):
        return 8 * self.block + (self.u - k)

    def half(self, k):
        return 4 * self.block + (self.u - k) // 2

    def group(self, k):
        return 2 * self.block + (self.u - k) // 4

    def slot(self, k):
        return (self.u - k) % 2

    def quarter(self, k):
        return (self.u - k) % 4

    def gslot(self, k):
        return (self.u - k) // 4 % 2

    def on(self, k):
        return not isinstance(self.block, int) or 0 <= self.n(k) < 64

    def past(self, k):
        return self.n(k) if not isinstance(self.block, int) else min(max(self.n(k), 0), 64)


NORM, INS, TOEP, KVS, CONV, SECOND, OUT, ROUTE = 0, 1, 4, 4, 5, 6, 9, 10
LOOPED = (3, 8)
BLOCKS = 10
STEPS = 74


def walk(eng, step, chain=None):
    for block in range(LOOPED[0]):
        for u in range(8):
            step(Step(block, u))
    with eng.Fori(0, LOOPED[1] - LOOPED[0]) as turn:
        block = turn + LOOPED[0]
        if chain:
            chain.restart(eng)
        for u in range(8):
            step(Step(block, u))
    if chain:
        chain.restart(eng)
    for block in range(LOOPED[1], BLOCKS):
        for u in range(8):
            if 8 * block + u < STEPS:
                step(Step(block, u))


def wait(eng, sem, value):
    if not isinstance(value, int) or value > 0:
        eng.wait_ge(sem, value)


def settle(pool, turns):
    pool.sem_inc(turns, 1)


def list_tile(pool, lists, toki, place, t, listed):
    for k in range(K):
        pool.indirect_dma_start(
            out=lists, out_offset=bass.IndirectOffsetOnAxis(ap=place[:, t, k:k + 1], axis=0),
            in_=toki[:, t:t + 1], in_offset=None).then_inc(listed, 16)


def load_weights(sp, raw, w_ld, gate, up, down, before_unit):
    for q in range(GU):
        before_unit(q)
        for src, c in ((gate, 0), (up, I)):
            sp.dma_start(raw[:, 2 * q:2 * q + 2, c:c + I],
                         src[2 * q * P:(2 * q + 2) * P, :].rearrange("(k p) i -> p k i", p=P))\
                .then_inc(w_ld[q], 16)
    for q in range(DN):
        before_unit(GU + q)
        sp.dma_start(raw[:, L // P + 2 * q:L // P + 2 * q + 2, :],
                     down[2 * q * P:(2 * q + 2) * P, :].rearrange("(k p) i -> p k i", p=P))\
            .then_inc(w_ld[GU + q], 16)


def expert_weights(A, e):
    one = slice(e, e + 1) if isinstance(e, int) else bass.ds(e, 1)
    return [A[k][one].rearrange("o a b -> (o a) b") for k in ("w_gate", "w_up", "w_down")]


def channel_rows(t, group, quarter):
    v = t.rearrange("(q b) (g c) l -> g q c b l", b=BT, c=CG)
    return v[bass.ds(group, 1), quarter].rearrange("o c b l -> (o c) b l")


def batch_rows(t, group, batch):
    return t[batch, bass.ds(group * CG, CG), :]


def mix_and_route(nc, A, keep):
    x, ctx, kern, dvec, rw, bias = A["x"], A["ctx"], A["kern"], A["dvec"], A["rw"], A["bias"]
    kpad, x2d, xnd, lists = A["kpad"], A["x2d"], A["xnd"], A["lists"]
    es = ExitStack()
    with es:
        def sb(name, shape, dt=F32):
            return es.enter_context(nc.sbuf_tensor(name, shape, dt))

        def sem(name):
            return es.enter_context(nc.semaphore(name))

        kT = [sb(f"kT{i}", [P, LB * B, CG]) for i in range(2)]
        qT = [sb(f"qT{i}", [P, LB * B, CG]) for i in range(2)]
        kv = sb("kv", [P, LB, HB, PAIRS])
        khi = [sb(f"khi{i}", [P, LB, NH], F32R) for i in range(2)]
        klo = [sb(f"klo{i}", [P, LB, NH], F32R) for i in range(2)]
        ysb = [sb(f"ysb{i}", [P, LB, HB, PAIRS]) for i in range(2)]
        prod = sb("prod", [P, LB * HB, HD, HD])
        traw = sb("traw", [P, L])
        thi = [sb(f"thi{i}", [P, L], F32R) for i in range(2)]
        tlo = [sb(f"tlo{i}", [P, L], F32R) for i in range(2)]
        xin = sb("xin", [P, L])
        cin = sb("cin", [P, L])
        xres = sb("xres", [P, L])
        xn2 = [sb(f"xn2{i}", [P, L]) for i in range(2)]
        x2T = sb("x2T", [P, LB, P])
        rws = sb("rws", [P, LB, E])
        biasb = sb("biasb", [P, E])
        st_in = sb("st_in", [P, 2, 6])
        mv_in = sb("mv_in", [P, 2])
        sd_in = sb("sd_in", [P, 3])
        st_out = sb("st_out", [P, 2, 6])
        mv_out = sb("mv_out", [P, 2])
        sd_out = sb("sd_out", [P, 3])
        lg = sb("lg", [P, RB, E])
        sc = sb("sc", [P, RB, E])
        sb_ = sb("sbias", [P, RB, E])
        msk = sb("msk", [P, RB, E])
        rep = sb("rep", [P, RB, E])
        chosen = sb("chosen", [P, RB, E])
        wn = sb("wn", [P, RB, E])
        key = sb("key", [P, RB, E])
        runs = sb("runs", [P, RB + 1, E])
        pm = sb("pm", [P, RB * EG, 4])
        gs = sb("gs", [P, RB, EG])
        gsel = sb("gsel", [P, RB, EG])
        top = sb("top", [P, RB, K])
        ws = sb("ws", [P, RB])
        tokf = sb("tokf", [P, RB])
        con, vslot, wpick, cnt = keep["con"], keep["vslot"], keep["wpick"], keep["cnt"]
        toki, place = keep["toki"], keep["place"]
        ident = con[:, C_ID:C_ID + P]
        kp = ysb[0][0:HEADS, :, :, :].rearrange("p a b c -> p (a b c)")[:, 0:P + L]
        zero_i = prod[:, 0:E, :, :].rearrange("p a b c -> p (a b c)").bitcast(I32)
        wide = prod[:, :, :, :].rearrange("p a b c -> p (a b c)")[:, 0:RB * K * E]\
            .rearrange("p (t k e) -> p t k e", t=RB, k=K)
        cmp8 = prod[:, :, :, :].rearrange("p a b c -> p (a b c)")[:, 0:2 * RB * EG * EG]\
            .rearrange("p (s t g h) -> p s t g h", s=2, t=RB, g=EG)

        def of_half(t, s, k, half):
            h = s.quarter(k)
            return t[s.gslot(k)][:, :, :].rearrange("p (m b) c -> p m b c", m=LB)[
                :, :, half * HB:(half + 1) * HB, HD * h:HD * h + HD]

        pr = prod[:, :, :, :].rearrange("p (m b) j i -> p m b j i", m=LB)

        yps = [es.enter_context(nc.psum_tensor(f"yps{i}", [P, 2, 512], F32)) for i in range(2)]
        ps0 = es.enter_context(nc.psum_tensor("ps0", [P, 2 * 512], F32))
        ps1 = es.enter_context(nc.psum_tensor("ps1", [P, 2 * 512], F32))

        setup_ld, kp_zero, kp_ready = sem("setup_ld"), sem("kp_zero"), sem("kp_ready")
        kpad_st, lists_st = sem("kpad_st"), sem("lists_st")
        x_ld, c_ld, t_ld = sem("x_ld"), sem("c_ld"), sem("t_ld")
        r_ld = sem("r_ld")
        x2_st, xn_st = sem("x2_st"), [sem(f"xn_st{i}") for i in range(2)]
        var_in, sqrt_in, scale_in, normed = sem("var_in"), sem("sqrt_in"), sem("scale_in"), sem("normed")
        var_out, sqrt_out, scale_out, normed2 = (sem("var_out"), sem("sqrt_out"), sem("scale_out"),
                                                 sem("normed2"))
        toep_mm, toep_high, toep_low = sem("toep_mm"), sem("toep_high"), sem("toep_low")
        kv_high, kv_low = [sem(f"kv_high{i}") for i in range(2)], [sem(f"kv_low{i}") for i in range(2)]
        xin_mm, xin_copied = sem("xin_mm"), sem("xin_copied")
        ctx_mm, ctx_copied = sem("ctx_mm"), sem("ctx_copied")
        kv_built = [sem(f"kv_built{i}") for i in range(2)]
        y_mm, y_copied = sem("y_mm"), sem("y_copied")
        first_done = [sem(f"first_done{i}") for i in range(2)]
        summed = [sem(f"summed{i}") for i in range(2)]
        out_mm, out_added = sem("out_mm"), sem("out_added")
        x2T_mm, x2T_copied = sem("x2T_mm"), sem("x2T_copied")
        lg_mm, lg_copied, scored = sem("lg_mm"), sem("lg_copied"), sem("scored")
        chose, rank_mm, rank_used = sem("chose"), sem("rank_mm"), sem("rank_used")
        placed, listed, place_free = sem("placed"), sem("listed"), sem("place_free")
        dve_seq, pool_turns = sem("dve_seq"), sem("pool_turns")

        block = es.enter_context(nc.Block())

        @block.sync
        def _(sp):
            sp.dma_start(kp[:, P - 1:P - 1 + L], kern).then_inc(setup_ld, 16)
            sp.dma_start(sd_in[0:HEADS, 0:1], dvec.rearrange("(h o) -> h o", o=1)).then_inc(setup_ld, 16)
            sp.dma_start(con[:, :], A["con"]).then_inc(setup_ld, 16)
            sp.dma_start(rws[:, :, :], rw.rearrange("(k p) e -> p k e", p=P)).then_inc(setup_ld, 16)
            sp.dma_start(biasb[:, :], bias.rearrange("(o e) -> o e", o=1).to_broadcast([P, E]))\
                .then_inc(setup_ld, 16)
            sp.wait_ge(kp_zero, 2)
            sp.dma_start(lists[0:E * LIST, :].rearrange("(p n) o -> p (n o)", p=P), zero_i)\
                .then_inc(lists_st, 16)
            sp.dma_start(lists[E * LIST:, :].rearrange("(p n) o -> p (n o)", p=P),
                         A["tokens"].rearrange("(p n) o -> p (n o)", p=P)).then_inc(lists_st, 16)
            sp.wait_ge(kp_ready, 1)
            sp.dma_start(kpad, kp).then_inc(kpad_st, 16)
            sp.wait_ge(kpad_st, 16)

            def step(s):
                k = TOEP - 1
                if s.on(k):
                    wait(sp, toep_mm, s.n(k))
                    src = bass.AP(tensor=kpad.tensor, offset=s.n(k) * (L + P),
                                  ap=[[1, P], [1, L]])
                    sp.dma_start(traw[:, :], src).then_inc(t_ld, 16)
                if s.on(NORM):
                    wait(sp, ctx_mm, s.n(NORM))
                    sp.dma_start(cin[:, :], channel_rows(ctx, s.group(NORM), s.quarter(NORM)))\
                        .then_inc(c_ld, 16)
                    wait(sp, xin_mm, s.n(NORM))
                    sp.dma_start(xin[:, :], channel_rows(x, s.group(NORM), s.quarter(NORM)))\
                        .then_inc(x_ld, 16)
                if s.on(OUT):
                    sp.wait_ge(normed2, s.n(OUT) + 1)
                    sp.dma_start(x2d[bass.ds(s.n(OUT) * P, P), :], xres[:, :]).then_inc(x2_st, 16)
                    sp.dma_start(xnd[bass.ds(s.n(OUT) * P, P), :], xn2[s.slot(OUT)][:, :])\
                        .then_inc(xn_st[s.slot(OUT)], 16)
                k = OUT - 1
                if s.on(k):
                    wait(sp, x2_st, 16 * s.n(k))
                    for b in range(BT):
                        sp.dma_start(xres[b * CG:(b + 1) * CG, :],
                                     batch_rows(x, s.group(k), s.quarter(k) * BT + b))\
                            .then_inc(r_ld, 16)

            walk(sp, step)
            sp.wait_ge(x2_st, 16 * NTILE)
            for i in range(2):
                sp.wait_ge(xn_st[i], 16 * NTILE // 2)

        @block.gpsimd
        def _(pool):
            def kv_lower(s, k, half):
                if not s.on(k):
                    return
                n = s.n(k)
                pool.wait_ge(kv_high[half], n + 1)
                pool.tensor_tensor(klo[half][:, :, :], kv[:, :, :, :].rearrange("p m b c -> p m (b c)"),
                                   khi[half][:, :, :].bitcast(F32), ALU.subtract).then_inc(kv_low[half], 1)

            def first_products(s, k, half):
                if not s.on(k):
                    return
                n, y, q = s.n(k), ysb[half], of_half(qT, s, k, half)
                pool.wait_ge(y_copied, 8 * n + 4 * half + 4)
                pool.wait_ge(xin_copied, TPG * (s.group(k) + 1))
                if half == 0:
                    wait(pool, summed[1], n)
                else:
                    pool.wait_ge(summed[0], n + 1)
                if half == 1 and routes(s, 2):
                    pool.wait_ge(chose, s.block - 1)
                if half == 1 and routes(s, 4):
                    pool.wait_ge(placed, s.block - 1)
                pool.tensor_tensor(pr[:, :, :, 0:HD, 0], y[:, :, :, 0:HD],
                                   q[:, :, :, 0:1].to_broadcast([P, LB, HB, HD]), ALU.mult)
                pool.tensor_tensor(pr[:, :, :, 0, 1:HD], y[:, :, :, 1:HD],
                                   q[:, :, :, 1:HD], ALU.mult).then_inc(first_done[half], 1)

            def step(s):
                first_products(s, SECOND, 1)
                kv_lower(s, CONV, 1)
                if 4 <= s.u and routes(s, s.u):
                    list_tokens(s.block - 2, (s.u - 4,))
                if s.u < 3 and routes(s, s.u, 3):
                    list_tokens(s.block - 3, ((4,), (5,), (6, 7))[s.u])
                kv_lower(s, KVS, 0)
                first_products(s, CONV, 0)

            def list_tokens(r, tiles):
                pool.wait_ge(placed, r + 1)
                settle(pool, pool_turns)
                for t in tiles:
                    list_tile(pool, lists, toki, place, t, listed)
                if RB - 1 in tiles:
                    pool.wait_ge(listed, 16 * RB * K * (r + 1))
                    pool.sem_inc(place_free, 1)

            pool.sem_inc(place_free, 1)
            pool.wait_ge(lists_st, 32)
            walk(pool, step)
            list_tokens(NTILE // RB - 2, (6, 7))

        @block.scalar
        def _(act):
            def copy_y(s, j):
                if not s.on(CONV):
                    return
                n, half, q = s.n(CONV), j // 4, j % 4
                if q == 0:
                    wait(act, summed[half], n)
                act.wait_ge(y_mm, 8 * n + j + 1)
                act.activation(ysb[half][:, 2 * q:2 * q + 2, :, :].rearrange("p m b c -> p m (b c)"),
                               yps[j % 2][:, :, 0:NH], ACT.Copy).then_inc(y_copied, 1)

            def kv_higher(s, k, half):
                if not s.on(k):
                    return
                n = s.n(k)
                act.wait_ge(kv_built[half], n + 1)
                if not isinstance(n, int) or n > 0:
                    act.wait_ge(y_mm, 8 * (n - 1) + 4 * half + 4)
                act.activation(khi[half][:, :, :], kv[:, :, :, :].rearrange("p m b c -> p m (b c)"), ACT.Copy).then_inc(kv_high[half], 1)

            def copy_tile(s, ps, dst):
                q = s.quarter(INS)
                v = dst[s.gslot(INS)][:, :, :].rearrange("p (m b) c -> p m b c", m=LB)
                return act.activation(v[:, :, q * BT:(q + 1) * BT, :],
                                      ps[:, :].rearrange("p (m c b) -> p m b c", m=LB, b=BT), ACT.Copy)

            def step(s):
                if s.on(INS):
                    act.wait_ge(ctx_mm, s.n(INS) + 1)
                    if not isinstance(s.block, int) or s.group(INS) >= 2:
                        act.wait_ge(kv_built[1], HPG * (s.group(INS) - 1))
                    copy_tile(s, ps1, kT).then_inc(ctx_copied, 1)
                copy_y(s, 0)
                kv_higher(s, CONV, 1)
                copy_y(s, 1)
                if s.on(INS):
                    act.wait_ge(scale_in, s.n(INS) + 1)
                    act.activation(xin[:, :], xin[:, :], ACT.Identity,
                                   bias=sd_in[:, 2:3], scale=sd_in[:, 1:2]).then_inc(normed, 1)
                if s.on(TOEP):
                    n = s.n(TOEP)
                    act.wait_ge(toep_mm, n + 1)
                    if not isinstance(n, int) or n > 1:
                        act.wait_ge(y_mm, 8 * (n - 1))
                    act.activation(thi[s.slot(TOEP)][:, :], ps0[:, :], ACT.Copy).then_inc(toep_high, 1)
                copy_y(s, 2)
                copy_y(s, 3)
                kv_higher(s, KVS, 0)
                copy_y(s, 4)
                if s.on(OUT):
                    act.wait_ge(var_out, s.n(OUT) + 1)
                    act.activation(sd_out[:, 0:1], mv_out[:, 1:2], ACT.Sqrt,
                                   bias=con[:, C_EPS:C_EPS + 1]).then_inc(sqrt_out, 1)
                copy_y(s, 5)
                if s.on(OUT):
                    act.wait_ge(scale_out, s.n(OUT) + 1)
                    wait(act, xn_st[s.slot(OUT)], 16 * s.half(OUT))
                    wait(act, x2T_mm, s.past(OUT + 1))
                    act.activation(xn2[s.slot(OUT)][:, :], xres[:, :], ACT.Identity,
                                   bias=sd_out[:, 2:3], scale=sd_out[:, 1:2]).then_inc(normed2, 1)
                if s.on(INS):
                    act.wait_ge(xin_mm, s.n(INS) + 1)
                    copy_tile(s, ps0, qT).then_inc(xin_copied, 1)
                copy_y(s, 6)
                if s.on(ROUTE):
                    act.wait_ge(x2T_mm, s.n(ROUTE) + 1)
                    act.activation(x2T[:, :, :].rearrange("p k t -> p (k t)"), ps1[:, :], ACT.Copy)\
                        .then_inc(x2T_copied, 1)
                copy_y(s, 7)
                if s.on(ROUTE):
                    act.wait_ge(lg_mm, s.n(ROUTE) + 1)
                    act.activation(lg[:, (s.u - ROUTE) % RB, :], ps0[:, 0:E], ACT.Copy)\
                        .then_inc(lg_copied, 1)
                if s.on(NORM):
                    act.wait_ge(var_in, s.n(NORM) + 1)
                    act.activation(sd_in[:, 0:1], mv_in[:, 1:2], ACT.Sqrt,
                                   bias=con[:, C_EPS:C_EPS + 1]).then_inc(sqrt_in, 1)
                if routes(s, 1):
                    act.wait_ge(lg_copied, s.n(ROUTE) + 1)
                    act.activation(sc[:, :, :], lg[:, :, :], ACT.Sigmoid).then_inc(scored, 1)

            act.wait_ge(setup_ld, 80)
            walk(act, step)

        @block.vector
        def _(dve):
            seq = Chain(dve_seq)

            def link(ins):
                seq.link(dve, ins)

            def statistics(src, st, mv):
                dve.bn_stats(st[:, 0, :], src[:, 0:L // 2])
                link(dve.bn_stats(st[:, 1, :], src[:, L // 2:L]))
                return dve.bn_aggr(mv[:, :], st[:, :, :].rearrange("p a b -> p (a b)"))

            def scale_and_shift(sd, mv):
                link(dve.reciprocal(sd[:, 1:2], sd[:, 0:1]))
                return dve.tensor_scalar(sd[:, 2:3], mv[:, 0:1], sd[:, 1:2], -1.0, ALU.mult, ALU.mult)

            def times_queries(s, k, half):
                n = s.n(k)
                y, q = ysb[half], of_half(qT, s, k, half)
                dve.wait_ge(y_copied, 8 * n + 4 * half + 4)
                dve.wait_ge(xin_copied, TPG * (s.group(k) + 1))
                at = HD
                for i in range(1, HD):
                    m = HD - i
                    last = dve.tensor_tensor(pr[:, :, :, i:HD, i], y[:, :, :, at:at + m],
                                             q[:, :, :, i:i + 1].to_broadcast([P, LB, HB, m]), ALU.mult)
                    if m > 1:
                        last = dve.tensor_tensor(pr[:, :, :, i, i + 1:HD], y[:, :, :, at + 1:at + m],
                                                 q[:, :, :, i + 1:HD], ALU.mult)
                    at += m
                link(last)
                dve.wait_ge(first_done[half], n + 1)
                dve.tensor_reduce(q, pr, AXX, ALU.add).then_inc(summed[half], 1)
                dve.wait_ge(summed[half], n + 1)

            def pair_products(s, k, half):
                if not s.on(k):
                    return
                n, kk = s.n(k), of_half(kT, s, k, half)
                dve.wait_ge(ctx_copied, TPG * (s.group(k) + 1))
                wait(dve, kv_low[1 - half], n + half)
                at = 0
                for i in range(HD):
                    m = HD - i
                    last = dve.tensor_tensor(kv[:, :, :, at:at + m], kk[:, :, :, i:HD],
                                             kk[:, :, :, i:i + 1].to_broadcast([P, LB, HB, m]), ALU.mult)
                    at += m
                last.then_inc(kv_built[half], 1)

            def step(s):
                if routes(s, 2):
                    choose(s.block - 2)
                if routes(s, 3):
                    count(s.block - 2)
                if s.on(SECOND):
                    times_queries(s, SECOND, 1)
                if s.on(TOEP):
                    dve.wait_ge(toep_high, s.n(TOEP) + 1)
                    dve.tensor_tensor(tlo[s.slot(TOEP)][:, :], ps0[:, :],
                                      thi[s.slot(TOEP)][:, :].bitcast(F32), ALU.subtract).then_inc(toep_low, 1)
                pair_products(s, KVS, 0)
                if s.on(OUT):
                    n, xr = s.n(OUT), xres
                    dve.wait_ge(r_ld, 16 * BT * (s.n(OUT) + 1))
                    dve.wait_ge(out_mm, n + 1)
                    dve.tensor_tensor(xr[:, :], xr[:, :], ps1[:, :], ALU.add).then_inc(out_added, 1)
                    dve.wait_ge(out_added, n + 1)
                    wait(dve, normed2, n)
                    statistics(xr, st_out, mv_out).then_inc(var_out, 1)
                if s.on(OUT):
                    dve.wait_ge(sqrt_out, n + 1)
                    scale_and_shift(sd_out, mv_out).then_inc(scale_out, 1)
                if s.on(CONV):
                    times_queries(s, CONV, 0)
                if s.on(NORM):
                    dve.wait_ge(x_ld, 16 * (s.n(NORM) + 1))
                    wait(dve, normed, s.n(NORM))
                    statistics(xin, st_in, mv_in).then_inc(var_in, 1)
                pair_products(s, KVS, 1)
                if s.on(NORM):
                    dve.wait_ge(sqrt_in, s.n(NORM) + 1)
                    scale_and_shift(sd_in, mv_in).then_inc(scale_in, 1)
                if routes(s, 3):
                    assign(s.block - 2)

            def choose(r):
                dve.wait_ge(scored, r + 1)
                link(dve.tensor_tensor(sb_[:, :, :], sc[:, :, :],
                                       biasb[:, :].rearrange("p (o e) -> p o e", o=1).to_broadcast([P, RB, E]), ALU.add))
                two = sb_[:, :, :].rearrange("p t (g a c) -> p (t g) a c", a=2, c=2)
                dve.tensor_tensor(pm[:, :, 0:2], two[:, :, :, 0], two[:, :, :, 1], ALU.max)
                link(dve.tensor_tensor(pm[:, :, 2:4], two[:, :, :, 0], two[:, :, :, 1], ALU.min))
                g = gs[:, :, :].rearrange("p t g -> p (t g)")
                gb = gsel[:, :, :].rearrange("p t g -> p (t g)")
                dve.tensor_tensor(g, pm[:, :, 0], pm[:, :, 1], ALU.max)
                dve.tensor_tensor(gb, pm[:, :, 0], pm[:, :, 1], ALU.min)
                link(dve.tensor_tensor(pm[:, :, 2], pm[:, :, 2], pm[:, :, 3], ALU.max))
                link(dve.tensor_tensor(gb, gb, pm[:, :, 2], ALU.max))
                link(dve.tensor_tensor(g, g, gb, ALU.add))
                other = gs[:, :, :].rearrange("p t (o g) -> p t o g", o=1).to_broadcast([P, RB, EG, EG])
                own = gs[:, :, :].rearrange("p t (g o) -> p t g o", o=1).to_broadcast([P, RB, EG, EG])
                dve.tensor_tensor(cmp8[:, 0], other, own, ALU.is_gt)
                link(dve.tensor_tensor(cmp8[:, 1], other, own, ALU.is_equal))
                before = con[:, C_GT:C_GT + EG * EG].rearrange("p (o g h) -> p o g h", o=1, g=EG)\
                    .to_broadcast([P, RB, EG, EG])
                link(dve.tensor_tensor(cmp8[:, 1], cmp8[:, 1], before, ALU.mult))
                link(dve.tensor_tensor(cmp8[:, 0], cmp8[:, 0], cmp8[:, 1], ALU.add))
                link(dve.tensor_reduce(gsel[:, :, :], cmp8[:, 0], AXX, ALU.add))
                link(dve.tensor_scalar(gsel[:, :, :], gsel[:, :, :], float(TKG), None, ALU.is_lt))
                link(dve.tensor_tensor(msk[:, :, :].rearrange("p t (g c) -> p (t g) c", c=GSZ),
                                       sb_[:, :, :].rearrange("p t (g c) -> p (t g) c", c=GSZ),
                                       gsel[:, :, :].rearrange("p t (g o) -> p (t g) o", o=1)
                                       .to_broadcast([P, RB * EG, GSZ]), ALU.mult))
                link(dve.tensor_scalar(msk[:, :, :], msk[:, :, :], 0.0, None, ALU.add))
                for t in range(RB):
                    last = dve.max(top[:, t, :], msk[:, t, :])
                link(last)
                for t in range(RB):
                    last = dve.match_replace(rep[:, t, :], top[:, t, :], msk[:, t, :], -3e38)
                link(last)
                dve.tensor_tensor(chosen[:, :, :], rep[:, :, :], msk[:, :, :], ALU.not_equal)\
                    .then_inc(chose, 1)
                dve.wait_ge(chose, r + 1)
                link(dve.tensor_tensor(wn[:, :, :], sc[:, :, :], chosen[:, :, :], ALU.mult))
                link(dve.tensor_reduce(ws[:, :], wn[:, :, :], AXX, ALU.add))
                link(dve.reciprocal(ws[:, :], ws[:, :]))
                link(dve.tensor_tensor(wn[:, :, :], wn[:, :, :],
                                       ws[:, :].rearrange("p (t o) -> p t o", o=1).to_broadcast([P, RB, E]),
                                       ALU.mult))
                link(dve.tensor_scalar(wn[:, :, :], wn[:, :, :], SCALE, None, ALU.mult))

            def count(r):
                dve.wait_ge(rank_mm, r + 1)
                total = ps0[:, 512:512 + RB * E].rearrange("p (t e) -> p t e", e=E)
                link(dve.tensor_copy(runs[:, 0, :], cnt[:, :]))
                for t in range(RB):
                    link(dve.tensor_tensor(runs[:, t + 1, :], runs[:, t, :], total[:, t, :], ALU.add))
                dve.tensor_copy(cnt[:, :], runs[:, RB, :])
                link(dve.tensor_tensor(key[:, :, :], runs[:, 0:RB, :],
                                       ps0[:, 0:RB * E].rearrange("p (t e) -> p t e", e=E), ALU.add))
                dve.tensor_tensor(key[:, :, :], key[:, :, :],
                                  con[:, C_EB:C_EB + E].rearrange("p (o e) -> p o e", o=1)
                                  .to_broadcast([P, RB, E]), ALU.add).then_inc(rank_used, 1)
                dve.wait_ge(rank_used, r + 2)

            def assign(r):
                link(dve.scalar_tensor_tensor(out=key[:, :, :], in0=key[:, :, :], scalar=1.0,
                                              in1=chosen[:, :, :], op0=ALU.add, op1=ALU.mult))
                for t in range(RB):
                    last = dve.max(top[:, t, :], key[:, t, :])
                link(last)
                link(dve.tensor_tensor(wide, key[:, :, :].rearrange("p t (o e) -> p t o e", o=1)
                                       .to_broadcast([P, RB, K, E]),
                                       top[:, :, :].rearrange("p t (k o) -> p t k o", o=1)
                                       .to_broadcast([P, RB, K, E]), ALU.is_equal))
                link(dve.tensor_tensor(wide, wide, wn[:, :, :].rearrange("p t (o e) -> p t o e", o=1)
                                       .to_broadcast([P, RB, K, E]), ALU.mult))
                dve.tensor_reduce(wpick[:, bass.ds(r * RB, RB), :], wide, AXX, ALU.add)
                link(dve.tensor_scalar(vslot[:, bass.ds(r * RB, RB), :], top[:, :, :], -1.0, None, ALU.add))
                dve.wait_ge(place_free, r + 1)
                link(dve.tensor_scalar(place[:, :, :], top[:, :, :], -1.0, None, ALU.add))
                link(dve.tensor_copy(toki[:, :], tokf[:, :]))
                dve.tensor_scalar(tokf[:, :], tokf[:, :], float(RB * P), None, ALU.add)\
                    .then_inc(placed, 1)

            dve.sem_inc(rank_used, 1)
            dve.memset(kp[:, 0:P - 1], 0.0).then_inc(kp_zero, 1)
            dve.memset(zero_i, 0).then_inc(kp_zero, 1)
            dve.memset(kp[:, P - 1 + L:P + L], 0.0)
            dve.memset(cnt[:, :], 0.0)
            dve.wait_ge(setup_ld, 80)
            link(dve.tensor_copy(tokf[:, :], con[:, C_TOK:C_TOK + RB]))
            dve.tensor_tensor(kp[:, P - 1:P], kp[:, P - 1:P], sd_in[0:HEADS, 0:1], ALU.add)\
                .then_inc(kp_ready, 1)
            dve.wait_ge(kp_ready, 1)
            dve.wait_ge(kpad_st, 16)
            dve.wait_ge(lists_st, 32)
            walk(dve, step, seq)
            choose(NTILE // RB - 1)
            count(NTILE // RB - 1)
            assign(NTILE // RB - 1)

        @block.tensor
        def _(pe):
            def free0(s, toep_now=0, xin_now=0):
                wait(pe, toep_low, s.past(TOEP) + toep_now)
                wait(pe, xin_copied, s.past(INS) + xin_now)
                wait(pe, lg_copied, s.past(ROUTE))
                done = s.block - 2 + (s.u > 2)
                pe.wait_ge(rank_used, 1 + (done if not isinstance(s.block, int) else max(done, 0)))

            def free1(s, ctx_now=0, out_now=0):
                wait(pe, ctx_copied, s.past(INS) + ctx_now)
                wait(pe, out_added, s.past(OUT) + out_now)
                wait(pe, x2T_copied, s.past(ROUTE))

            def conv(s, j):
                if not s.on(CONV):
                    return
                n, sl, half, q = s.n(CONV), s.slot(CONV), j // 4, j % 4
                if q == 0:
                    pe.wait_ge(kv_low[half], n + 1)
                    pe.wait_ge(toep_low, n + 1)
                m = 8 * n + j
                wait(pe, y_copied, max(m - 1, 0) if isinstance(m, int) else m - 1)
                for lb in (2 * q, 2 * q + 1):
                    for d in range(lb + 1):
                        c = slice(d * P, (d + 1) * P)
                        passes = ((thi, khi), (thi, klo), (tlo, khi))
                        for i, (tt, kk) in enumerate(passes):
                            last = pe.matmul(yps[j % 2][:, lb % 2, 0:NH], tt[sl][:, c], kk[half][:, lb - d, :],
                                             start=(d == 0 and i == 0), stop=(d == lb and i == 2))
                last.then_inc(y_mm, 1)

            def step(s):
                if s.on(INS):
                    pe.wait_ge(c_ld, 16 * (s.n(INS) + 1))
                    free1(s)
                    for m in range(LB):
                        last = pe.transpose(ps1[:, m * P:(m + 1) * P],
                                            cin[:, m * P:(m + 1) * P], ident)
                    last.then_inc(ctx_mm, 1)
                conv(s, 0)
                conv(s, 1)
                if s.on(TOEP):
                    pe.wait_ge(t_ld, 16 * (s.n(TOEP) + 1))
                    free0(s)
                    for i in range(2):
                        last = pe.matmul(ps0[:, i * 512:(i + 1) * 512], con[:, C_REV:C_REV + P],
                                         traw[:, i * 512:(i + 1) * 512], start=True, stop=True)
                    last.then_inc(toep_mm, 1)
                conv(s, 2)
                conv(s, 3)
                if s.on(OUT):
                    pe.wait_ge(summed[1], HPG * (s.group(OUT) + 1))
                    free1(s, ctx_now=int(s.on(INS)))
                    o = qT[s.gslot(OUT)][:, :, :].rearrange("p (m q b) c -> p m q (b c)", m=LB, b=BT)
                    for m in range(LB):
                        last = pe.transpose(ps1[:, m * P:(m + 1) * P], o[:, m, s.quarter(OUT)], ident)
                    last.then_inc(out_mm, 1)
                conv(s, 4)
                conv(s, 5)
                if s.on(INS):
                    pe.wait_ge(normed, s.n(INS) + 1)
                    free0(s, toep_now=int(s.on(TOEP)))
                    for m in range(LB):
                        last = pe.transpose(ps0[:, m * P:(m + 1) * P],
                                            xin[:, m * P:(m + 1) * P], ident)
                    last.then_inc(xin_mm, 1)
                conv(s, 6)
                if s.on(ROUTE):
                    pe.wait_ge(normed2, s.n(ROUTE) + 1)
                    free1(s, ctx_now=int(s.on(INS)), out_now=int(s.on(OUT)))
                    for m in range(LB):
                        last = pe.transpose(ps1[:, m * P:(m + 1) * P],
                                            xn2[s.slot(ROUTE)][:, m * P:(m + 1) * P], ident)
                    last.then_inc(x2T_mm, 1)
                conv(s, 7)
                if s.on(ROUTE):
                    pe.wait_ge(x2T_copied, s.n(ROUTE) + 1)
                    free0(s, toep_now=int(s.on(TOEP)), xin_now=int(s.on(INS)))
                    for m in range(LB):
                        last = pe.matmul(ps0[:, 0:E], x2T[:, m, :], rws[:, m, :],
                                         start=(m == 0), stop=(m == LB - 1))
                    last.then_inc(lg_mm, 1)
                if routes(s, 2):
                    ranks(s, s.block - 2)

            def ranks(s, r):
                pe.wait_ge(chose, r + 1)
                wait(pe, toep_low, s.past(TOEP) + int(s.on(TOEP)))
                wait(pe, xin_copied, s.past(INS) + int(s.on(INS)))
                wait(pe, lg_copied, s.past(ROUTE) + int(s.on(ROUTE)))
                m = chosen[:, :, :].rearrange("p t e -> p (t e)")
                pe.matmul(ps0[:, 0:RB * E], con[:, C_TRI:C_TRI + P], m, start=True, stop=True)
                pe.matmul(ps0[:, 512:512 + RB * E], con[:, C_ONE:C_ONE + P], m, start=True, stop=True)\
                    .then_inc(rank_mm, 1)

            pe.wait_ge(setup_ld, 80)
            walk(pe, step)
            ranks(Step(BLOCKS, 0), NTILE // RB - 1)


def routes(s, u, since=2):
    return s.u == u and (not isinstance(s.block, int) or since <= s.block)



def plan(nc, A, keep):
    es = ExitStack()
    with es:
        def sb(name, shape, dt=F32):
            return es.enter_context(nc.sbuf_tensor(name, shape, dt))

        con, vslot, cnt, table = (keep[k] for k in ("con", "vslot", "cnt", "table"))
        orow = keep["orow"]
        fields = sb("fields", [P, TCOLS * P, OFIELDS], I32)
        over = sb("over", [P, EXPERT_TILES])
        rows = sb("rows", [P, EXPERT_TILES])
        nti = sb("nti", [P, E], I32)
        nt = sb("nt", [P, NE])
        tend = sb("tend", [P, NE])
        shift = sb("shift", [P, E])
        spot = sb("spot", [P, NTILE * K])
        part = sb("part", [P, NTILE * K])
        past = sb("past", [P, TCOLS, NE - 1])
        pastn = sb("pastn", [P, TCOLS, NE - 1])
        ex = sb("ex", [P, TCOLS])
        at = sb("at", [P, TCOLS])
        rowf = sb("rowf", [P, TCOLS])
        start = sb("start", [P, TCOLS])
        end = sb("end", [P, TCOLS])
        tab = sb("tab", [P, TCOLS, FIELDS], I32)
        otab = sb("otab", [P, TCOLS, OFIELDS], I32)
        seq_sem = es.enter_context(nc.semaphore("plan_seq"))
        tab_ready = es.enter_context(nc.semaphore("tab_ready"))
        tab_st = es.enter_context(nc.semaphore("tab_st"))
        tab_ld = es.enter_context(nc.semaphore("tab_ld"))
        last_listed = es.enter_context(nc.semaphore("last_listed"))
        block = es.enter_context(nc.Block())

        @block.gpsimd
        def _(pool):
            for t in range(RB):
                list_tile(pool, A["lists"], keep["toki"], keep["place"], t, last_listed)
            pool.wait_ge(last_listed, 16 * RB * K)

        @block.sync
        def _(sp):
            load_weights(sp, keep["raw"], keep["w_ld"], *expert_weights(A, 0), lambda unit: None)
            sp.wait_ge(tab_ready, 1)
            sp.dma_start(A["tabd"].rearrange("(c p k) -> p c k", p=P, k=FIELDS), tab[:, :, :])\
                .then_inc(tab_st, 16)
            sp.dma_start(A["otabd"].rearrange("(c p k) -> p c k", p=P, k=OFIELDS), otab[:, :, :])\
                .then_inc(tab_st, 16)
            sp.wait_ge(tab_st, 32)
            sp.dma_start(table[:, :], A["tabd"][0:TILES * FIELDS].rearrange("(o n) -> o n", o=1)).then_inc(tab_ld, 16)
            sp.dma_start(fields[:, :, :].rearrange("p t k -> p (t k)"),
                         A["otabd"].rearrange("(o n) -> o n", o=1).to_broadcast([P, TCOLS * P * OFIELDS]))\
                .then_inc(tab_ld, 16)
            sp.wait_ge(tab_ld, 32)

        @block.vector
        def _(dve):
            seq = Chain(seq_sem)

            def link(ins):
                seq.link(dve, ins)

            link(dve.tensor_scalar(nti[:, :], cnt[:, :], float(P - 1), None, ALU.add))
            link(dve.tensor_scalar(nti[:, :], nti[:, :], P.bit_length() - 1, None, ALU.logical_shift_right))
            link(dve.tensor_scalar(nt[:, 0:E], nti[:, :], 1.0, None, ALU.max))
            link(dve.tensor_tensor_scan(tend[:, 0:E], con[:, C_ONE:C_ONE + E], nt[:, 0:E], 0.0,
                                        ALU.mult, ALU.add))
            link(dve.tensor_scalar(shift[:, :], cnt[:, :], float(-LIST), None, ALU.add))
            link(dve.tensor_scalar(nt[:, E - 1:E], tend[:, E - 2:E - 1], -1.0, float(SH0), ALU.mult, ALU.add))
            dve.memset(nt[:, E:E + 1], float(NTILE))
            dve.memset(tend[:, E - 1:E], float(SH0))
            link(dve.memset(tend[:, E:E + 1], float(SH1)))
            tn = con[:, C_T:C_T + TCOLS].rearrange("p (c o) -> p c o", o=1).to_broadcast([P, TCOLS, NE - 1])
            ends = tend[:, 0:NE - 1].rearrange("p (o e) -> p o e", o=1).to_broadcast([P, TCOLS, NE - 1])
            nts = nt[:, 0:NE - 1].rearrange("p (o e) -> p o e", o=1).to_broadcast([P, TCOLS, NE - 1])
            link(dve.tensor_tensor(past[:, :, :], tn, ends, ALU.is_ge))
            dve.tensor_reduce(ex[:, :], past[:, :, :], AXX, ALU.add)
            link(dve.tensor_tensor(pastn[:, :, :], past[:, :, :], nts, ALU.mult))
            link(dve.tensor_reduce(at[:, :], pastn[:, :, :], AXX, ALU.add))

            def tokens_of(first):
                c = cnt[:, first:first + E - 1].rearrange("p (o e) -> p o e", o=1).to_broadcast([P, TCOLS, E - 1])
                return dve.tensor_tensor(pastn[:, :, 0:E - 1], past[:, :, 0:E - 1], c, ALU.mult)

            link(tokens_of(0))
            link(dve.tensor_reduce(start[:, :], pastn[:, :, 0:E - 1], AXX, ALU.add))
            link(tokens_of(1))
            link(dve.tensor_reduce(end[:, :], pastn[:, :, 0:E - 1], AXX, ALU.add))
            link(dve.tensor_scalar(otab[:, :, F_END], end[:, :], cnt[:, 0:1], None, ALU.add))
            link(dve.tensor_tensor(at[:, :], con[:, C_T:C_T + TCOLS], at[:, :], ALU.subtract))
            link(dve.scalar_tensor_tensor(out=otab[:, :, F_START], in0=at[:, :], scalar=float(P),
                                          in1=start[:, :], op0=ALU.mult, op1=ALU.add))
            link(dve.tensor_scalar(at[:, :], at[:, :], float(LROWS - 1), None, ALU.min))
            link(dve.tensor_scalar(rowf[:, :], ex[:, :], float(E), float(LROWS), ALU.min, ALU.mult))
            dve.tensor_copy(tab[:, :, F_EXPERT], ex[:, :])
            dve.tensor_scalar(tab[:, :, F_FIRST], at[:, :], 0.0, None, ALU.is_equal)
            dve.tensor_tensor(tab[:, :, F_ROW], rowf[:, :], at[:, :], ALU.add).then_inc(tab_ready, 1)
            v = vslot[:, :, :].rearrange("p t k -> p (t k)")
            link(dve.tensor_copy(spot[:, :], v))
            for e in range(1, E):
                link(dve.tensor_scalar(part[:, :], v, float(LIST * e), shift[:, e - 1:e], ALU.is_ge, ALU.mult))
                link(dve.tensor_tensor(spot[:, :], spot[:, :], part[:, :], ALU.add))
            link(dve.tensor_copy(v.bitcast(I32), spot[:, :]))
            dve.wait_ge(tab_ld, 32)
            f = fields[:, 0:EXPERT_TILES, :]
            link(dve.tensor_scalar(rows[:, :], f[:, :, F_START], con[:, C_T:C_T + 1], None, ALU.add))
            link(dve.tensor_tensor(over[:, :], rows[:, :], f[:, :, F_END], ALU.is_ge))
            link(dve.scalar_tensor_tensor(out=orow[:, :], in0=over[:, :], scalar=float(2 * NTOK * K),
                                          in1=rows[:, :], op0=ALU.mult, op1=ALU.add))


class Tile:

    def __init__(self, first, u=0, turn=0):
        self.first, self.u, self.turn, self.fixed = first, u, turn, isinstance(turn, int)

    def part(self, k=0):
        t = self.first + self.u + k
        return None if t < SH0 else int(t >= SH1)

    def n(self, k=0):
        return self.first + self.u + k + 2 * self.turn

    def slot(self, k=0):
        return (self.first + self.u + k) % 2

    def half(self, k=0):
        return (self.first + self.u + k) // 2 + self.turn

    def on(self, k=0):
        return not self.fixed or 0 <= self.n(k) < TILES


PEELED = 3
ROUTED_TURNS = (SH0 + 1 - PEELED) // 2
HALF_TURNS = NTILE // 2 - 1
LAST_TURNS = NTILE // 2 - 3


def walk_tiles(eng, tile, before_sums=None):
    for t in range(PEELED):
        tile(Tile(t))
    with eng.Fori(0, ROUTED_TURNS) as turn:
        for u in range(2):
            tile(Tile(PEELED, u, turn))
    if before_sums:
        before_sums()
    tile(Tile(SH0 + 1))
    with eng.Fori(0, HALF_TURNS) as turn:
        for u in range(2):
            tile(Tile(SH0 + 2, u, turn))
    for t in (SH1, SH1 + 1):
        tile(Tile(t))
    with eng.Fori(0, LAST_TURNS) as turn:
        for u in range(2):
            tile(Tile(SH1 + 2, u, turn))
    for t in range(SH1 + 2 + 2 * LAST_TURNS, TILES + 1):
        tile(Tile(t))


def feed_forward(nc, A, keep):
    xnd, x2d, lists, yd, out = A["xnd"], A["x2d"], A["lists"], A["yd"], A["out"]
    shd = A["shd"]
    es = ExitStack()
    with es:
        def sb(name, shape, dt=F32):
            return es.enter_context(nc.sbuf_tensor(name, shape, dt))

        def sem(name):
            return es.enter_context(nc.semaphore(name))

        con, wpick, table = (keep[k] for k in ("con", "wpick", "table"))
        pick = keep["vslot"][:, :, :].bitcast(I32)
        orow = keep["orow"]
        ident = con[:, C_ID:C_ID + P]
        KX, KH = L // P, I // P
        whi = sb("whi", [P, KX + KH, 2 * I], F32R)
        wlo = sb("wlo", [P, KX + KH, 2 * I], F32R)
        raw, w_ld = keep["raw"], keep["w_ld"]
        idx = [sb(f"idx{i}", [P, 1], I32) for i in range(2)]
        gidx = [sb(f"gidx{i}", [P, K // 2], I32) for i in range(2)]
        yidx = [sb(f"yidx{i}", [P, 1], I32) for i in range(2)]
        xg = [sb(f"xg{i}", [P, L]) for i in range(2)]
        xhi, xlo = sb("xhi", [P, KX, P], F32R), sb("xlo", [P, KX, P], F32R)
        hb = sb("hb", [P, I])
        hhi, hlo = sb("hhi", [P, KH, P], F32R), sb("hlo", [P, KH, P], F32R)
        yrow = [sb(f"yrow{i}", [P, L]) for i in range(2)]
        picked = [sb(f"picked{k}", [P, L]) for k in range(K // 2)]

        gps = es.enter_context(nc.psum_tensor("gps", [P, 512], F32))
        ups = es.enter_context(nc.psum_tensor("ups", [P, 512], F32))
        xps = es.enter_context(nc.psum_tensor("xps", [P, 1024], F32))
        hps = es.enter_context(nc.psum_tensor("hps", [P, 512], F32))
        yps = es.enter_context(nc.psum_tensor("yps", [P, 1024], F32))

        hi_gu, lo_gu, hi_dn, lo_dn = sem("hi_gu"), sem("lo_gu"), sem("hi_dn"), sem("lo_dn")
        idx_ld = [sem(f"idx_ld{i}") for i in range(2)]
        x_ld = [sem(f"xg_ld{i}") for i in range(2)]
        y_st = [sem(f"y_st{i}") for i in range(2)]
        half_st, out_st = [sem(f"half_st{i}") for i in range(2)], [sem(f"out_st{i}") for i in range(2)]
        acc_ld = [sem(f"acc_ld{i}") for i in range(2)]
        pick_ld = [sem(f"pick_ld{k}") for k in range(K // 2)]
        pool_turns = sem("pool_turns2")
        gidx_ready, yidx_ready = sem("gidx_ready"), sem("yidx_ready")
        gu_mm, xT_mm, down_mm, hT_mm = sem("gu_mm"), sem("xT_mm"), sem("down_mm"), sem("hT_mm")
        silu_done, h_done = sem("silu_done"), sem("h_done")
        x_hi, x_lo, h_hi, h_lo = sem("x_hi"), sem("x_lo"), sem("h_hi"), sem("h_lo")
        y_act, y_dve, pick_used = sem("y_act"), sem("y_dve"), sem("pick_used")
        block = es.enter_context(nc.Block())

        def entry(eng, t, what, most):
            return eng.value_load(table[0:1, bass.ds(t * FIELDS + what, 1)], min_val=0, max_val=most)

        def expert(eng, t):
            return 0 if isinstance(t, int) and t == 0 else entry(eng, t, F_EXPERT, NE - 1)

        @block.sync
        def _(sp):
            def load(e, weights):
                def before_unit(q):
                    if q < GU:
                        sp.wait_ge(lo_gu, GU * (e - 1) + q + 1)
                    else:
                        sp.wait_ge(lo_dn, DN * (e - 1) + q - GU + 1)
                load_weights(sp, raw, w_ld, *weights, before_unit)

            with sp.Fori(1, E) as e:
                load(e, expert_weights(A, e))
            for s in range(NE - E):
                cols = slice(s * I, (s + 1) * I)
                load(E + s, (A["sw_gate"][:, cols], A["sw_up"][:, cols], A["sw_down"][cols, :]))

            sp.wait_ge(y_st[0], 16 * SH0 // 2)
            sp.wait_ge(y_st[1], 16 * SH0 // 2)

            def fetch(src, n, i):
                sp.dma_start(yrow[i][:, :], src[bass.ds(n * P, P), :]).then_inc(acc_ld[i], 16)

            for i in range(2):
                fetch(x2d, i, i)
            with sp.Fori(1, NTILE // 2) as turn:
                for i in range(2):
                    sp.wait_ge(half_st[i], 16 * turn)
                    fetch(x2d, 2 * turn + i, i)
            for i in range(2):
                sp.wait_ge(half_st[i], 16 * NTILE // 2)
                fetch(shd, i, i)
            with sp.Fori(1, NTILE // 2) as turn:
                for i in range(2):
                    sp.wait_ge(out_st[i], 16 * BT * turn)
                    fetch(shd, 2 * turn + i, i)

        @block.gpsimd
        def _(pool):
            def load_list(t, slot, turns):
                row = entry(pool, t, F_ROW, (E + 1) * LROWS - 1)
                wait(pool, x_ld[slot], 16 * turns)
                pool.dma_start(idx[slot][:, :], lists[bass.ds(row * P, P), :]).then_inc(idx_ld[slot], 16)

            def gather(t, slot, turns):
                wait(pool, xT_mm, t - 1 if not isinstance(t, int) else max(t - 1, 0))
                pool.wait_ge(idx_ld[slot], 16 * (turns + 1))
                settle(pool, pool_turns)
                pool.indirect_dma_start(out=xg[slot][:, :], out_offset=None, in_=xnd,
                                        in_offset=bass.IndirectOffsetOnAxis(ap=idx[slot][:, 0:1], axis=0))\
                    .then_inc(x_ld[slot], 16)

            def fetch_picks(m, slot, half):
                if not isinstance(m, int) or m > 0:
                    pool.wait_ge(pick_used, K // 2 * (m - 1) + 1)
                pool.tensor_copy(gidx[slot][:, :],
                                 pick[:, bass.ds(m - half * NTILE, 1), K // 2 * half:K // 2 * (half + 1)]
                                 .rearrange("p o k -> p (o k)")).then_inc(gidx_ready, 1)
                pool.wait_ge(gidx_ready, m + 1)
                for k in range(K // 2):
                    if not isinstance(m, int) or m > 0:
                        pool.wait_ge(pick_used, K // 2 * (m - 1) + k + 1)
                    settle(pool, pool_turns)
                    pool.indirect_dma_start(out=picked[k][:, :], out_offset=None, in_=yd,
                                            in_offset=bass.IndirectOffsetOnAxis(ap=gidx[slot][:, k:k + 1], axis=0))\
                        .then_inc(pick_ld[k], 16)

            def tile(c):
                if c.part(-1) is not None:
                    fetch_picks(c.n(-1 - SH0), c.slot(-1 - SH0), c.part(-1))
                if c.on(3):
                    load_list(c.n(3), c.slot(3), c.half(3))
                if c.on(2):
                    gather(c.n(2), c.slot(2), c.half(2))
                if c.part(-1) is None and c.on(-1):
                    store(c, c.slot(-1))

            def store(c, i):
                wait(pool, y_st[i], 16 * c.half(-1))
                pool.tensor_copy(yidx[i][:, :], orow[:, bass.ds(c.n(-1), 1)]).then_inc(yidx_ready, 1)
                pool.wait_ge(yidx_ready, c.n())
                pool.wait_ge(y_act, c.n())
                pool.wait_ge(y_dve, c.n())
                settle(pool, pool_turns)
                pool.indirect_dma_start(out=yd, in_=yrow[i][:, :], in_offset=None,
                                        out_offset=bass.IndirectOffsetOnAxis(ap=yidx[i][:, 0:1], axis=0),
                                        bounds_check=NTOK * K - 1, oob_is_err=False).then_inc(y_st[i], 16)

            def before_sums():
                pool.wait_ge(y_st[0], 16 * SH0 // 2)
                pool.wait_ge(y_st[1], 16 * SH0 // 2)

            for t in range(3):
                if t == 2:
                    gather(0, 0, 0)
                    gather(1, 1, 0)
                load_list(t, t % 2, t // 2)
            walk_tiles(pool, tile, before_sums)

        @block.scalar
        def _(act):
            def split_gu(e):
                for q in range(GU):
                    act.wait_ge(w_ld[q], 32 * (e + 1))
                    act.activation(whi[:, 2 * q:2 * q + 2, :], raw[:, 2 * q:2 * q + 2, :], ACT.Copy)\
                        .then_inc(hi_gu, 1)

            def split_dn(e):
                for q in range(DN):
                    act.wait_ge(w_ld[GU + q], 16 * (e + 1))
                    act.activation(whi[:, KX + 2 * q:KX + 2 * q + 2, :], raw[:, KX + 2 * q:KX + 2 * q + 2, :],
                                   ACT.Copy).then_inc(hi_dn, 1)

            def x_high(t):
                act.wait_ge(xT_mm, t + 1)
                act.activation(xhi[:, :, :].rearrange("p k t -> p (k t)"), xps[:, :], ACT.Copy).then_inc(x_hi, 1)

            def tile(c):
                t = c.n()
                store_sum(c)
                if c.on():
                    act.wait_ge(gu_mm, t + 1)
                    wait(act, hT_mm, t)
                    act.activation(hb[:, :], gps[:, :], ACT.Silu).then_inc(silu_done, 1)
                if c.on(1):
                    x_high(c.n(1))
                    if c.part(-1) != 1:
                        with act.If(entry(act, c.n(1), F_FIRST, 1) == 1):
                            split_gu(entry(act, c.n(1), F_EXPERT, NE - 1))
                if c.on(-1) and c.part(-1) is None:
                    act.wait_ge(down_mm, t)
                    wait(act, y_st[c.slot(-1)], 16 * c.half(-1))
                    act.activation(yrow[c.slot(-1)][:, 0:512], yps[:, 0:512], ACT.Copy).then_inc(y_act, 1)
                if c.on():
                    act.wait_ge(hT_mm, t + 1)
                    act.activation(hhi[:, :, :].rearrange("p k t -> p (k t)"), hps[:, :], ACT.Copy).then_inc(h_hi, 1)
                if c.fixed and t == 0:
                    split_dn(0)
                elif c.part(-1) != 1:
                    with act.If(entry(act, t, F_FIRST, 1) == 1):
                        e = entry(act, t, F_EXPERT, NE - 1)
                        act.wait_ge(down_mm, t)
                        split_dn(e)

            def store_sum(c):
                half = c.part(-2)
                if half is None:
                    return
                n, i = c.n(-2 - (SH1 if half else SH0)), c.slot(-2)
                act.wait_ge(y_dve, c.n(-1))
                if half == 0:
                    act.dma_start(shd[bass.ds(n * P, P), :], yrow[i][:, :]).then_inc(half_st[i], 16)
                    return
                for b in range(BT):
                    dst = out[bass.ds(n % TPG * BT + b, 1), bass.ds(n // TPG * CG, CG), :]
                    act.dma_start(dst.rearrange("o c l -> (o c) l"), yrow[i][b * CG:(b + 1) * CG, :])\
                        .then_inc(out_st[i], 16)

            split_gu(0)
            x_high(0)
            walk_tiles(act, tile)
            store_sum(Tile(TILES + 1))
            for i in range(2):
                act.wait_ge(out_st[i], 16 * BT * NTILE // 2)

        @block.vector
        def _(dve):
            def low(dst, src, hi):
                return dve.tensor_tensor(dst, src, hi.bitcast(F32), ALU.subtract)

            def split_gu(e):
                for q in range(GU):
                    r = slice(2 * q, 2 * q + 2)
                    dve.wait_ge(hi_gu, GU * e + q + 1)
                    low(wlo[:, r, :], raw[:, r, :], whi[:, r, :]).then_inc(lo_gu, 1)

            def split_dn(e):
                for q in range(DN):
                    r = slice(KX + 2 * q, KX + 2 * q + 2)
                    dve.wait_ge(hi_dn, DN * e + q + 1)
                    low(wlo[:, r, :], raw[:, r, :], whi[:, r, :]).then_inc(lo_dn, 1)

            def x_low(t):
                dve.wait_ge(x_hi, t + 1)
                low(xlo[:, :, :].rearrange("p k t -> p (k t)"), xps[:, :],
                    xhi[:, :, :].rearrange("p k t -> p (k t)")).then_inc(x_lo, 1)

            def add_picks(m, i, turns, half):
                dve.wait_ge(acc_ld[i], 16 * (turns + 1))
                for k in range(K // 2):
                    dve.wait_ge(pick_ld[k], 16 * (m + 1))
                    at = K // 2 * half + k
                    dve.scalar_tensor_tensor(
                        out=yrow[i][:, :], in0=picked[k][:, :],
                        scalar=wpick[:, bass.ds(m - half * NTILE, 1), at:at + 1].rearrange("p o k -> p (o k)"),
                        in1=yrow[i][:, :], op0=ALU.mult, op1=ALU.add).then_inc(pick_used, 1)
                    dve.wait_ge(pick_used, K // 2 * m + k + 1)

            def tile(c):
                t = c.n()
                if c.on():
                    dve.wait_ge(silu_done, t + 1)
                    dve.tensor_tensor(hb[:, :], hb[:, :], ups[:, :], ALU.mult).then_inc(h_done, 1)
                if c.on(1):
                    x_low(c.n(1))
                    if c.part(-1) != 1:
                        with dve.If(entry(dve, c.n(1), F_FIRST, 1) == 1):
                            split_gu(entry(dve, c.n(1), F_EXPERT, NE - 1))
                i = c.slot(-1)
                if c.part(-1) is not None:
                    add_picks(c.n(-1 - SH0), i, c.half(-1 - SH0), c.part(-1))
                    dve.wait_ge(down_mm, t)
                    dve.tensor_tensor(yrow[i][:, :], yrow[i][:, :], yps[:, :], ALU.add).then_inc(y_dve, 1)
                elif c.on(-1):
                    dve.wait_ge(down_mm, t)
                    wait(dve, y_st[i], 16 * c.half(-1))
                    dve.tensor_copy(yrow[i][:, 512:1024], yps[:, 512:1024]).then_inc(y_dve, 1)
                if c.on():
                    dve.wait_ge(h_hi, t + 1)
                    low(hlo[:, :, :].rearrange("p k t -> p (k t)"), hps[:, :],
                        hhi[:, :, :].rearrange("p k t -> p (k t)")).then_inc(h_lo, 1)
                if c.fixed and t == 0:
                    split_dn(0)
                elif c.part(-1) != 1:
                    with dve.If(entry(dve, t, F_FIRST, 1) == 1):
                        split_dn(entry(dve, t, F_EXPERT, NE - 1))

            split_gu(0)
            x_low(0)
            walk_tiles(dve, tile)

        @block.tensor
        def _(pe):
            def three(hi, lo, chunk, outs, first, last_one):
                passes = ((hi, whi), (hi, wlo), (lo, whi))
                for n, (rows, w) in enumerate(passes):
                    for i, ps in enumerate(outs):
                        ins = pe.matmul(ps, rows, w[:, chunk, i * 512:(i + 1) * 512],
                                        start=first and n == 0, stop=last_one and n == 2)
                return ins

            def transpose_rows(t, slot, turns):
                pe.wait_ge(x_ld[slot], 16 * (turns + 1))
                for m in range(KX):
                    last = pe.transpose(xps[:, m * P:(m + 1) * P], xg[slot][:, m * P:(m + 1) * P], ident)
                last.then_inc(xT_mm, 1)

            def tile(c):
                t = c.n()
                if c.on():
                    e = expert(pe, t)
                    pe.wait_ge(x_lo, t + 1)
                    wait(pe, h_done, t)
                    for m in range(KX):
                        if m % 2 == 0:
                            pe.wait_ge(lo_gu, GU * e + m // 2 + 1)
                        last = three(xhi[:, m, :], xlo[:, m, :], m, (gps[:, :], ups[:, :]),
                                     m == 0, m == KX - 1)
                    last.then_inc(gu_mm, 1)
                if c.on(1):
                    transpose_rows(c.n(1), c.slot(1), c.half(1))
                if c.on(-1):
                    e = expert(pe, c.n(-1))
                    pe.wait_ge(h_lo, t)
                    if c.part(-2) is None:
                        wait(pe, y_act, c.n(-1))
                    wait(pe, y_dve, c.n(-1))
                    for m in range(KH):
                        if m % 2 == 0:
                            pe.wait_ge(lo_dn, DN * e + m // 2 + 1)
                        last = three(hhi[:, m, :], hlo[:, m, :], KX + m,
                                     (yps[:, 0:512], yps[:, 512:1024]), m == 0, m == KH - 1)
                    last.then_inc(down_mm, 1)
                if c.on():
                    pe.wait_ge(h_done, t + 1)
                    for m in range(KH):
                        last = pe.transpose(hps[:, m * P:(m + 1) * P], hb[:, m * P:(m + 1) * P], ident)
                    last.then_inc(hT_mm, 1)

            transpose_rows(0, 0, 0)
            walk_tiles(pe, tile)


def program(nc, x, ctx, kern, dvec, rw, bias, w_gate, w_up, w_down, sw_gate, sw_up, sw_down,
            con_d, tokens, out):
    A = dict(x=x, ctx=ctx, kern=kern, dvec=dvec, rw=rw, bias=bias, w_gate=w_gate, w_up=w_up,
             w_down=w_down, sw_gate=sw_gate, sw_up=sw_up, sw_down=sw_down, con=con_d, tokens=tokens, out=out)
    A["kpad"] = nc.dram_tensor("kpad", (HEADS, L + P), F32).ap()
    A["x2d"] = nc.dram_tensor("x2d", (NTOK, L), F32).ap()
    A["xnd"] = nc.dram_tensor("xnd", (NTOK, L), F32).ap()
    A["lists"] = nc.dram_tensor("lists", ((E + 1) * LIST, 1), I32).ap()
    A["yd"] = nc.dram_tensor("yd", (NTOK * K, L), F32).ap()
    A["shd"] = nc.dram_tensor("shd", (NTOK, L), F32).ap()
    A["tabd"] = nc.dram_tensor("tabd", (TCOLS * P * FIELDS,), I32).ap()
    A["otabd"] = nc.dram_tensor("otabd", (TCOLS * P * OFIELDS,), I32).ap()
    with ExitStack() as es:
        def sb(name, shape, dt=F32):
            return es.enter_context(nc.sbuf_tensor(name, shape, dt))
        keep = dict(con=sb("con_sb", [P, C_N]), vslot=sb("vslot", [P, NTILE, K]),
                    wpick=sb("wpick", [P, NTILE, K]), cnt=sb("cnt", [P, E]),
                    toki=sb("toki", [P, RB], I32), place=sb("place", [P, RB, K], I32))
        mix_and_route(nc, A, keep)
        keep["table"] = sb("table", [1, TILES * FIELDS], I32)
        keep["orow"] = sb("orow", [P, EXPERT_TILES], I32)
        keep["raw"] = sb("raw", [P, (L + I) // P, 2 * I])
        keep["w_ld"] = [es.enter_context(nc.semaphore(f"w_ld{q}")) for q in range(UNITS)]
        plan(nc, A, keep)
        feed_forward(nc, A, keep)


_INS = ["x", "ctx_2048", "L0_xattn_ssm_kernel", "L0_xattn_D", "L0_ffn_router_w", "L0_ffn_router_bias",
        "L0_ffn_w_gate", "L0_ffn_w_up", "L0_ffn_w_down", "L0_ffn_sw_gate", "L0_ffn_sw_up", "L0_ffn_sw_down"]


def kernel(**inputs):
    import numpy as _np
    import concourse.bacc as _bacc
    from concourse.bass_utils import run_bass_kernel_spmd as _run

    nc = _bacc.Bacc("TRN2", target_bir_lowering=False, num_devices=1)
    con, tokens = constants()
    arrays, args = {}, []
    for name, a in [(n, inputs[n]) for n in _INS] + [("con", con), ("tokens", tokens)]:
        a = _np.ascontiguousarray(a)
        arrays[f"in_{name}_dram"] = a
        args.append(nc.dram_tensor(f"in_{name}_dram", a.shape, mybir.dt.from_np(a.dtype),
                                   kind="ExternalInput").ap())
    args.append(nc.dram_tensor("out_dram", (B, CH, L), F32, kind="ExternalOutput").ap())
    program(nc, *args)
    return _run(nc, [arrays], core_ids=[0]).results[0]["out_dram"]
```
